# Optimizing a Trainium2 kernel written in Bass

```python
import numpy as np
import jax
import jax.numpy as jnp

def _softmax(x, axis=-1):
    return jax.nn.softmax(x, axis=axis)

def _gelu(x):
    return jax.nn.gelu(x, approximate=True)

def _silu(x):
    return jax.nn.silu(x)

def _sigmoid(x):
    return jax.nn.sigmoid(x)

def _layernorm(x, axis=-1, eps=1e-05):
    m = jnp.mean(x, axis=axis, keepdims=True)
    v = jnp.var(x, axis=axis, keepdims=True)
    return (x - m) / jnp.sqrt(v + eps)

def _scatter_add(tgt, idx, src, axis=0):
    return tgt.at[idx].add(src)

def _segment_sum(src, seg, n):
    return jax.ops.segment_sum(src, seg, n)
kernel_name = 'mk_decoder_preln_d1_seqx_r8_92eac3'

def setup_inputs(seed: int=0):
    np.random.seed(seed)
    _w = jnp.asarray

    def _rec_inputs():
        import jax
        import jax.numpy as jnp
        _rk = jax.random.key(seed)
        x = 7.22e-05 + 1 * jax.random.normal(jax.random.fold_in(_rk, 1), (16, 256, 128), jnp.float32)
        _lenS = 256 - jax.random.randint(jax.random.fold_in(_rk, 7), (16,), 0, max(1, 256 // 4) + 1, jnp.int32)
        _lenS2 = 64 - jax.random.randint(jax.random.fold_in(_rk, 8), (16,), 0, max(1, 64 // 4) + 1, jnp.int32)
        _ctx_1024P = jax.random.normal(jax.random.fold_in(_rk, 11), (16, 16, 128), jnp.float32)
        _ctx_1024c = jax.random.dirichlet(jax.random.fold_in(_rk, 511), 0.3 * jnp.ones((16,), jnp.float32), (16, 64))
        _ctx_1024t = jnp.einsum('bsk,bkd->bsd', _ctx_1024c, _ctx_1024P)
        _ctx_1024t = _ctx_1024t * jax.lax.rsqrt(jnp.mean(jnp.square(_ctx_1024t)) + 1e-12) * 0.953939
        ctx_1024 = 4.13588e-05 + 0.999923 * (_ctx_1024t + 0.3 * jax.random.normal(jax.random.fold_in(_rk, 611), (16, 64, 128), jnp.float32))
        _validS = jnp.arange(256)[None, :] < _lenS[:, None]
        _validS2 = jnp.arange(64)[None, :] < _lenS2[:, None]
        _causal = jnp.tril(jnp.ones((256, 256), dtype=bool))
        mask_BxSxS2_ik1 = jnp.where(jnp.broadcast_to(_validS2[:, None, :], (16, 256, 64)), 1, 0).astype(jnp.int32)
        return (x, ctx_1024, mask_BxSxS2_ik1)
    x, ctx_1024, mask_BxSxS2_ik1 = _rec_inputs()

    def _L0_attn_setup():
        import jax, jax.numpy as jnp
        import numpy as np
        B, S, D_MODEL, H = (4, 256, 128, 16)
        D_K = D_MODEL // H
        key = jax.random.key(seed)
        kx, kq, kk, kv, ko = jax.random.split(key, 5)
        scale = 1.0 / np.sqrt(D_MODEL)
        return {'x': jax.random.normal(kx, (B, S, D_MODEL), dtype=jnp.float32), 'W_q': jax.random.normal(kq, (D_MODEL, D_MODEL), dtype=jnp.float32) * scale, 'W_k': jax.random.normal(kk, (D_MODEL, D_MODEL), dtype=jnp.float32) * scale, 'W_v': jax.random.normal(kv, (D_MODEL, D_MODEL), dtype=jnp.float32) * scale, 'W_out': jax.random.normal(ko, (D_MODEL, D_MODEL), dtype=jnp.float32) * scale}
    _L0_attn_all = _L0_attn_setup()
    _L0_attn_in = {k: v for k, v in _L0_attn_all.items() if k in ('W_q', 'W_k', 'W_v', 'W_out')}
    del _L0_attn_all

    def _L0_xattn_setup():
        import jax, jax.numpy as jnp
        import numpy as np
        B, T, D = (4, 256, 128)
        H, DK, DV = (16, 64, 64)
        key = jax.random.key(seed)
        ks = jax.random.split(key, 12)
        s = 0.02
        return {'query': jax.random.normal(ks[0], (B, T, D), jnp.float32), 'key': jax.random.normal(ks[1], (B, T, D), jnp.float32), 'value': jax.random.normal(ks[2], (B, T, D), jnp.float32), 'mask': jax.random.randint(ks[3], (B, T, T), 0, 2, jnp.int32), 'Wq': jax.random.normal(ks[4], (H * DK, D), jnp.float32) * s, 'bq': jnp.zeros((H * DK,), jnp.float32), 'Wk': jax.random.normal(ks[5], (H * DK, D), jnp.float32) * s, 'bk': jnp.zeros((H * DK,), jnp.float32), 'Wv': jax.random.normal(ks[6], (H * DV, D), jnp.float32) * s, 'bv': jnp.zeros((H * DV,), jnp.float32), 'Wo': jax.random.normal(ks[7], (D, H * DV), jnp.float32) * s, 'bo': jnp.zeros((D,), jnp.float32)}
    _L0_xattn_all = _L0_xattn_setup()
    _L0_xattn_in = {k: v for k, v in _L0_xattn_all.items() if k in ('Wq', 'bq', 'Wk', 'bk', 'Wv', 'bv', 'Wo', 'bo')}
    del _L0_xattn_all

    def _L0_ffn_setup():
        import jax, jax.numpy as jnp
        import numpy as np
        B, S, H = (4, 256, 128)
        D_FF = 4 * H
        NUM_EXPERTS = 8
        TOP_K = 2
        key = jax.random.key(seed)
        ks = jax.random.split(key, 6)
        scale = 0.02
        return {'hidden_states': jax.random.normal(ks[0], (B, S, H), dtype=jnp.float32), 'w_router': jax.random.normal(ks[1], (NUM_EXPERTS, H), dtype=jnp.float32) * scale, 'w1': jax.random.normal(ks[2], (NUM_EXPERTS, D_FF, H), dtype=jnp.float32) * scale, 'b1': jnp.zeros((NUM_EXPERTS, D_FF), dtype=jnp.float32), 'w2': jax.random.normal(ks[3], (NUM_EXPERTS, H, D_FF), dtype=jnp.float32) * scale, 'b2': jnp.zeros((NUM_EXPERTS, H), dtype=jnp.float32)}
    _L0_ffn_all = _L0_ffn_setup()
    _L0_ffn_in = {k: v for k, v in _L0_ffn_all.items() if k in ('w_router', 'w1', 'b1', 'w2', 'b2')}
    del _L0_ffn_all
    return {'x': x, 'ctx_1024': ctx_1024, 'mask_BxSxS2_ik1': mask_BxSxS2_ik1, 'L0_attn_W_q': _L0_attn_in['W_q'], 'L0_attn_W_k': _L0_attn_in['W_k'], 'L0_attn_W_v': _L0_attn_in['W_v'], 'L0_attn_W_out': _L0_attn_in['W_out'], 'L0_xattn_Wq': _L0_xattn_in['Wq'], 'L0_xattn_bq': _L0_xattn_in['bq'], 'L0_xattn_Wk': _L0_xattn_in['Wk'], 'L0_xattn_bk': _L0_xattn_in['bk'], 'L0_xattn_Wv': _L0_xattn_in['Wv'], 'L0_xattn_bv': _L0_xattn_in['bv'], 'L0_xattn_Wo': _L0_xattn_in['Wo'], 'L0_xattn_bo': _L0_xattn_in['bo'], 'L0_ffn_w_router': _L0_ffn_in['w_router'], 'L0_ffn_w1': _L0_ffn_in['w1'], 'L0_ffn_b1': _L0_ffn_in['b1'], 'L0_ffn_w2': _L0_ffn_in['w2'], 'L0_ffn_b2': _L0_ffn_in['b2']}

def reference(x, ctx_1024, mask_BxSxS2_ik1, L0_attn_W_q, L0_attn_W_k, L0_attn_W_v, L0_attn_W_out, L0_xattn_Wq, L0_xattn_bq, L0_xattn_Wk, L0_xattn_bk, L0_xattn_Wv, L0_xattn_bv, L0_xattn_Wo, L0_xattn_bo, L0_ffn_w_router, L0_ffn_w1, L0_ffn_b1, L0_ffn_w2, L0_ffn_b2):
    import jax
    import jax.numpy as jnp

    def _L0_attn_ref(x, W_q, W_k, W_v, W_out):
        import jax, jax.numpy as jnp
        import numpy as np
        B, S, D_MODEL, H = (4, 256, 128, 16)
        D_K = D_MODEL // H
        Bx, Sx, D = x.shape
        q = (x @ W_q.T).reshape(Bx, Sx, H, D_K).transpose(0, 2, 1, 3)
        k = (x @ W_k.T).reshape(Bx, Sx, H, D_K).transpose(0, 2, 1, 3)
        v = (x @ W_v.T).reshape(Bx, Sx, H, D_K).transpose(0, 2, 1, 3)
        scores = jnp.einsum('bhsd,bhtd->bhst', q, k) / jnp.sqrt(jnp.float32(D_K))
        attn = jax.nn.softmax(scores, axis=-1)
        out = jnp.einsum('bhst,bhtd->bhsd', attn, v)
        out = out.transpose(0, 2, 1, 3).reshape(Bx, Sx, D)
        return out @ W_out.T

    def _L0_xattn_ref(query, key, value, mask, Wq, bq, Wk, bk, Wv, bv, Wo, bo):
        import jax, jax.numpy as jnp
        import numpy as np
        B, T, D = (4, 256, 128)
        H, DK, DV = (16, 64, 64)
        b = query.shape[0]
        q = (query @ Wq.T + bq).reshape(b, -1, H, DK).transpose(0, 2, 1, 3)
        k = (key @ Wk.T + bk).reshape(b, -1, H, DK).transpose(0, 2, 1, 3)
        v = (value @ Wv.T + bv).reshape(b, -1, H, DV).transpose(0, 2, 1, 3)
        scores = jnp.einsum('bhqd,bhkd->bhqk', q, k) / jnp.sqrt(jnp.float32(DK))
        m = mask[:, None, :, :] == 0
        scores = jnp.where(m, jnp.float32(-1e+20), scores)
        attn = jax.nn.softmax(scores, axis=-1)
        attn = jnp.where(m, 0.0, attn)
        x = jnp.einsum('bhqk,bhkd->bhqd', attn, v)
        x = x.transpose(0, 2, 1, 3).reshape(b, -1, H * DV)
        return x @ Wo.T + bo

    def _L0_ffn_ref(hidden_states, w_router, w1, b1, w2, b2):
        import jax, jax.numpy as jnp
        import numpy as np
        B, S, H = (4, 256, 128)
        D_FF = 4 * H
        NUM_EXPERTS = 8
        TOP_K = 2
        Bc, Sc, Hc = hidden_states.shape
        E = w_router.shape[0]
        dtype = hidden_states.dtype
        router_logits = jnp.einsum('bsh,eh->bse', hidden_states, w_router)
        topk_values, topk_indices = jax.lax.top_k(router_logits, TOP_K)
        topk_weights = jax.nn.softmax(topk_values.astype(jnp.float32), axis=-1).astype(dtype)
        combine = jnp.sum(jax.nn.one_hot(topk_indices, E, dtype=dtype) * topk_weights[..., None], axis=-2)
        flat = hidden_states.reshape(-1, Hc)
        cw = combine.reshape(-1, E)
        mixed = jnp.zeros_like(flat)
        for e in range(E):
            h1 = jax.nn.gelu(flat @ w1[e].T + b1[e], approximate=False)
            mixed = mixed + cw[:, e:e + 1] * (h1 @ w2[e].T + b2[e])
        return mixed.reshape(Bc, Sc, Hc)
    x = x + _L0_attn_ref(_layernorm(x, axis=-1), L0_attn_W_q, L0_attn_W_k, L0_attn_W_v, L0_attn_W_out)
    x = x + _L0_xattn_ref(_layernorm(x, axis=-1), ctx_1024, ctx_1024, mask_BxSxS2_ik1, L0_xattn_Wq, L0_xattn_bq, L0_xattn_Wk, L0_xattn_bk, L0_xattn_Wv, L0_xattn_bv, L0_xattn_Wo, L0_xattn_bo)
    x = x + _L0_ffn_ref(_layernorm(x, axis=-1), L0_ffn_w_router, L0_ffn_w1, L0_ffn_b1, L0_ffn_w2, L0_ffn_b2)
    return x

_drawn_inputs = setup_inputs


def setup_inputs(seed=0):
    import zlib

    import numpy as np

    out = dict(_drawn_inputs(seed))
    spreads = {'L0_xattn_bq': (0.0, 0.8),
     'L0_xattn_bk': (0.0, 0.8),
     'L0_xattn_bv': (0.0, 0.1),
     'L0_xattn_bo': (0.0, 0.1),
     'L0_ffn_b1': (0.0, 0.474),
     'L0_ffn_b2': (0.0, 0.1)}
    factors = {'L0_xattn_Wq': 8.0, 'L0_xattn_Wk': 8.0}
    for name, (base, spread) in spreads.items():
        noise = np.random.default_rng([zlib.crc32(name.encode()), seed]).standard_normal(out[name].shape)
        drawn = base * np.exp(spread * noise) if base else spread * noise
        out[name] = jnp.asarray(drawn.astype(out[name].dtype))
    for name, factor in factors.items():
        out[name] = (out[name] * factor).astype(out[name].dtype)
    return out
```

```python
from contextlib import ExitStack

import concourse.bass as bass
import concourse.mybir as mybir
import numpy as np

F32, F32R, BF16 = mybir.dt.float32, mybir.dt.float32r, mybir.dt.bfloat16
I32, U32 = mybir.dt.int32, mybir.dt.uint32
ALU, ACT, AX = mybir.AluOpType, mybir.ActivationFunctionType, mybir.AxisListType

P = 128
NB, S, D = 16, 256, 128
ST = S // P
NH, DK = 16, 8
T2, DX = 64, 64
NX = 16
NPAIR = NX // 2
NE, FF = 8, 512
FB = FF // P
NPIECE = 3
ROWS = NPIECE * NPIECE * DK
EPS = 1e-5
MASKED = -1e20
SCALE_A, SCALE_B = DK ** -0.5, DX ** -0.5
END = "end"


class Done:

    def __init__(self, sem, lead, count):
        self.sem, self.lead, self.count = sem, lead, count


class Plan:

    LEAD = {"A": 2, "B": 1, "C": 0, "W": 0}

    def __init__(self):
        self.per_batch = {}
        self.start()

    def start(self):
        self.counts, self.queues = {}, {}
        return self.queues

    def finish(self):
        for sem, n in self.counts.items():
            assert self.per_batch.setdefault(sem, n) == n, sem

    def step(self, engine, stage, make, after=(), sem=None, add=1, apart=False):
        sem = sem or f"{engine}_{stage}"
        self.counts[sem] = self.counts.get(sem, 0) + add
        self.queues.setdefault(engine, []).append((list(after), make, sem, add, self.LEAD[stage], apart))
        return Done(sem, self.LEAD[stage], self.counts[sem])

    def dma(self, engine, stage, name, make, after=()):
        return self.step(engine, stage, make, after, f"dma_{name}", 16)

    def emit(self, eng, queue, sems, j, looped, spare=None):
        passed = {}
        for after, make, sem, add, lead, apart in queue:
            waits = 0
            for d in after:
                if d is None or (not looped and j + d.lead < 0):
                    continue
                k = self.per_batch[d.sem]
                count = k if d.count == END else d.count
                if passed.get((d.sem, d.lead), 0) >= count:
                    continue
                passed[d.sem, d.lead] = count
                eng.wait_ge(sems[d.sem], j * k + (d.lead * k + count))
                waits += 1
            if apart and looped and waits:
                eng.memset(spare, 0.0)
            make(eng, j + lead).then_inc(sems[sem], add)


def layer_norm(plan, stage, x, out, stats, moments, rstd, half, after, free):
    def statistics(v, b):
        for n in range(ST):
            last = v.bn_stats(stats[:, n, :], x[:, n, :])
        return last

    def aggregate(v, b):
        for n in range(ST):
            last = v.bn_aggr(moments[:, n, :], stats[:, n, :])
        return last

    def normalise(v, b):
        for n in range(ST):
            last = v.tensor_scalar(out[:, n, :], x[:, n, :], moments[:, n, 0:1], rstd[:, n:n + 1],
                                   ALU.subtract, ALU.mult)
        return last

    t = plan.step("vector", stage, statistics, after)
    t = plan.step("vector", stage, aggregate, [t], apart=True)
    t = plan.step("vector", stage, lambda v, b: v.tensor_scalar(
        rstd[:, :], moments[:, :, 1], EPS, None, ALU.add), [t])
    t = plan.step("gpsimd", stage, lambda g, b: g.tensor_tensor(
        rstd[:, :], rstd[:, :], half[:, :], ALU.pow), [t])
    return plan.step("vector", stage, normalise, [t, *free])


def transpose_tiles(plan, stage, dst, src, ident, after):
    def make(pe, b):
        for n in range(ST):
            last = pe.transpose(dst[:, n * P:(n + 1) * P], src[:, n, :], ident[:, :])
        return last
    return plan.step("tensor", stage, make, after)


def three_passes(pe, out, w_hi, w_lo, x_hi, x_lo, stop=True):
    pe.matmul(out, w_hi, x_hi, start=True, stop=False)
    pe.matmul(out, w_hi, x_lo, start=False, stop=False)
    return pe.matmul(out, w_lo, x_hi, start=False, stop=stop)


def f32(ap):
    return ap.bitcast(F32)


def build(nc, x, ctx_t, mask, attn_w, xq, xk, xv, xo, xbias, bo, w_router, w1, b1, w2, b2, out):
    stack = ExitStack()
    with stack:
        def sb(name, shape, dt=F32, at=stack):
            return at.enter_context(nc.sbuf_tensor(name, shape, dt))

        def psum(name, shape):
            return stack.enter_context(nc.psum_tensor(name, shape, F32))

        def dram(name, shape, dt):
            return nc.dram_tensor(name, shape, dt, kind="Internal").ap()

        a_all = dram("a_all", [NB, P, NX * T2], F32)
        u_all = dram("u_all", [NB, P, NPAIR * D], F32)
        r_all = dram("r_all", [NPIECE, NB, NX, T2], BF16)
        parts_dram = dram("parts_dram", [2, NPIECE, P, S], BF16)

        big = [psum(f"big{n}", [P, 2 * 512]) for n in range(3)]
        small = [psum(f"small{n}", [P, 512]) for n in range(2)]

        ident = sb("ident", [P, P])
        minus_half = sb("minus_half", [P, ST])
        euler = sb("euler", [P, ST])
        spare = sb("spare", [1, 1])
        iota8 = sb("iota8", [P, NE])
        iota_i = sb("iota_i", [P, NE], I32)
        ones_row = sb("ones_row", [NPIECE, P], BF16)
        wqk_hi = sb("wqk_hi", [P, 2, P], F32R)
        wqk_lo = sb("wqk_lo", [P, 2, P], F32R)
        wv_wo = sb("wv_wo", [P, 2, P])
        bo_all = sb("bo_all", [P, D])
        wr = sb("wr", [P, NE])
        w1_hi = sb("w1_hi", [P, NE, FF], F32R)
        w1_lo = sb("w1_lo", [P, NE, FF], F32R)
        w2_sb = sb("w2_sb", [P, NE, FB, D])
        b1_sb = sb("b1_sb", [P, NE * FB])
        b2_sb = sb("b2_sb", [NE, D])

        with ExitStack() as temporary:
            once(nc, temporary, sb, big, small, locals())

        main(nc, stack, sb, big, small, locals())


def once(nc, temporary, sb_, big, small, g):
    def sb(name, shape, dt=F32):
        return sb_(name, shape, dt, temporary)

    ident, w1_hi, w1_lo = g["ident"], g["w1_hi"], g["w1_lo"]
    wqk_raw = sb("wqk_raw", [P, 2, P])
    w1_raw = sb("w1_raw", [P, NE // 2, FF])
    ctx = sb("ctx", [P, NB * T2])
    xw = {n: sb(f"{n}_sb", [DX, NX, D]) for n in ("xq", "xk", "xv", "xo")}
    xb = sb("xb_sb", [DX, 3, NX])
    bv_cols = sb("bv_cols", [DX, NX, T2])
    bqk = sb("bqk", [DX, NX])
    ones_col = sb("ones_col", [DX, 1])
    gt = sb("gt", [P, NX, D])
    hh = sb("hh", [P, 2, NPAIR, D])
    vecs = sb("vecs", [P, 2, NX])
    beta = sb("beta", [NX, 1])
    u_bias = sb("u_bias", [P, NPAIR * D])
    r_f = sb("r_f", [NX, NB * T2])
    r_rest = sb("r_rest", [NX, NB * T2])
    r_parts = sb("r_parts", [NX, NPIECE, NB * T2], BF16)
    stage_buf = [sb(f"stage_buf{n}", [P, NB // 2, 1024]) for n in range(2)]

    plan = Plan()
    queues = plan.start()

    def load(name, dst, src, engine="sync"):
        return plan.dma(engine, "W", name, lambda e, b: e.dma_start(dst, src))

    W = lambda engine, make, after=(): plan.step(engine, "W", make, after)

    got_xk = load("xk", xw["xk"][:, :, :], g["xk"])
    got_xq = load("xq", xw["xq"][:, :, :], g["xq"])
    got_ctx = load("ctx", ctx[:, :], g["ctx_t"])
    got_xb = load("xbias", xb[:, :, :], g["xbias"])
    got_xv = load("xv", xw["xv"][:, :, :], g["xv"])
    got_xo = load("xo", xw["xo"][:, :, :], g["xo"])
    got_wqk = load("wqk", wqk_raw[:, :, :], g["attn_w"][:, 0:2, :])
    load("rest", g["wv_wo"][:, :, :], g["attn_w"][:, 2:4, :])
    load("rest", g["bo_all"][:, :], g["bo"].partition_broadcast(P))
    load("rest", g["wr"][:, :], g["w_router"])
    load("rest", g["b1_sb"][:, :], g["b1"])
    load("rest", g["b2_sb"][:, :], g["b2"])
    got_w1 = load("w1", w1_raw[:, :, :], g["w1"][:, 0:NE // 2, :])
    got_rest = load("rest", g["w2_sb"][:, :, :, :], g["w2"])

    t = W("gpsimd", lambda e, b: e.memset(ident[:, :], 0.0))
    got_ident = W("gpsimd", lambda e, b: e.affine_select(
        out=ident[:, :], in_=ident[:, :], compare_op=ALU.not_equal, fill=1.0, base=0,
        pattern=[[-1, P]], channel_multiplier=1), [t])
    t = W("gpsimd", lambda e, b: e.iota(g["iota_i"][:, :], pattern=[[1, NE]], base=0, channel_multiplier=0))
    W("vector", lambda e, b: e.tensor_copy(g["iota8"][:, :], g["iota_i"][:, :]), [t])
    W("vector", lambda e, b: e.memset(g["minus_half"][:, :], -0.5))
    W("vector", lambda e, b: e.memset(g["euler"][:, :], float(np.e)))
    W("vector", lambda e, b: e.memset(g["ones_row"][:, :], 1.0))
    got_ones = W("vector", lambda e, b: e.memset(ones_col[:, :], 1.0))

    small_free = [None, None]
    turn = 0
    got_g = []
    for h0 in range(0, NX, 4):
        def fold(pe, b, h0=h0, dst=small[turn % 2]):
            for h in range(h0, h0 + 4):
                last = pe.matmul(dst[:, (h - h0) * D:(h - h0 + 1) * D], xw["xk"][:, h, :], xw["xq"][:, h, :],
                                 start=True, stop=True)
            return last
        t = W("tensor", fold, [got_xk, got_xq, small_free[turn % 2]])
        t = W("vector", lambda v, b, h0=h0, src=small[turn % 2]: v.tensor_copy(
            gt[:, h0:h0 + 4, :].rearrange("p h d -> p (h d)"), src[:, :]), [t])
        small_free[turn % 2] = t
        got_g.append(t)
        turn += 1

    def vectors(pe, b, dst=small[turn % 2]):
        for h in range(NX):
            pe.matmul(dst[:, h:h + 1], xw["xq"][:, h, :], xb[:, 1, h:h + 1], start=True, stop=True)
            last = pe.matmul(dst[:, NX + h:NX + h + 1], xw["xk"][:, h, :], xb[:, 0, h:h + 1],
                             start=True, stop=True)
        return last
    t = W("tensor", vectors, [got_xb, small_free[turn % 2]])
    got_vecs = small_free[turn % 2] = W("vector", lambda v, b, src=small[turn % 2]: v.tensor_copy(
        vecs[:, :, :].rearrange("p a h -> p (a h)"), src[:, 0:2 * NX]), [t])
    turn += 1
    t = W("vector", lambda v, b: v.tensor_tensor(bqk[:, :], xb[:, 0, :], xb[:, 1, :], ALU.mult), [got_xb])
    t = W("tensor", lambda pe, b, dst=small[turn % 2]: pe.matmul(
        dst[0:NX, 0:1], bqk[:, :], ones_col[:, :], start=True, stop=True), [t, got_ones, small_free[turn % 2]])
    got_beta = small_free[turn % 2] = W("vector", lambda v, b, src=small[turn % 2]: v.tensor_copy(
        beta[:, :], src[0:NX, 0:1]), [t])
    turn += 1

    for half in range(2):
        cols = slice(half * 512, half * 512 + 512)
        t = W("tensor", lambda pe, b, dst=small[turn % 2], cols=cols: pe.matmul(
            dst[0:NX, :], vecs[:, 1, :], ctx[:, cols], start=True, stop=True),
            [got_vecs, got_ctx, small_free[turn % 2]])
        t = W("vector", lambda v, b, src=small[turn % 2], cols=cols: v.tensor_scalar(
            r_f[:, cols], src[0:NX, :], beta[:, 0:1], None, ALU.add), [t, got_beta])
        small_free[turn % 2] = t
        turn += 1
    t = W("vector", lambda v, b: v.tensor_copy(r_parts[:, 0, :], r_f[:, :]), [t])
    t = W("vector", lambda v, b: v.tensor_tensor(r_rest[:, :], r_f[:, :], r_parts[:, 0, :], ALU.subtract), [t])
    t = W("vector", lambda v, b: v.tensor_copy(r_parts[:, 1, :], r_rest[:, :]), [t])
    t = W("vector", lambda v, b: v.tensor_tensor(r_parts[:, 2, :], r_rest[:, :], r_parts[:, 1, :],
                                                 ALU.subtract), [t])
    for p in range(NPIECE):
        plan.dma("sync", "W", "r_out", lambda e, b, p=p: e.dma_start(
            g["r_all"][p].rearrange("b h t -> h b t"),
            r_parts[:, p, :].rearrange("h (b t) -> h b t", b=NB)), [t])

    big_free = [None, None, None]
    lot = 0
    stored = [None, None]
    for half in range(2):
        buf = stage_buf[half]
        for h in range(0, NX, 2):
            def key_side(pe, b, h=h, half=half, dst=big[lot % 3]):
                for k in range(2):
                    last = pe.matmul(dst[:, k * 512:(k + 1) * 512], gt[:, h + k, :],
                                     ctx[:, half * 512:(half + 1) * 512], start=True, stop=True)
                return last
            t = W("tensor", key_side, [*got_g, got_ctx, big_free[lot % 3]])

            def keep(e, k, h=h, buf=buf, src=big[lot % 3]):
                to = buf[:, :, (h + k) * T2:(h + k + 1) * T2]
                of = src[:, k * 512:(k + 1) * 512].rearrange("p (b t) -> p b t", t=T2)
                return to, of, vecs[:, 0, h + k:h + k + 1]
            t1 = W("scalar", lambda a, b, keep=keep: a.activation(
                keep(a, 0)[0], keep(a, 0)[1], ACT.Identity, bias=keep(a, 0)[2]), [t, got_vecs])
            t2 = W("vector", lambda v, b, keep=keep: v.tensor_scalar(
                keep(v, 1)[0], keep(v, 1)[1], keep(v, 1)[2], None, ALU.add), [t, got_vecs, t1])
            big_free[lot % 3] = t2
            lot += 1
        stored[half] = plan.dma("sync", "W", f"a_out{half}", lambda e, b, half=half, buf=buf: e.dma_start(
            g["a_all"][half * NB // 2:(half + 1) * NB // 2].rearrange("b p n -> p b n"), buf[:, :, :]), [t1, t2])

    got_h = []
    for par in range(2):
        for q in range(0, NPAIR, 4):
            def fold_v(pe, b, par=par, q=q, dst=small[turn % 2]):
                for k in range(4):
                    h = 2 * (q + k) + par
                    last = pe.matmul(dst[:, k * D:(k + 1) * D], xw["xv"][:, h, :], xw["xo"][:, h, :],
                                     start=True, stop=True)
                return last
            t = W("tensor", fold_v, [got_xv, got_xo, small_free[turn % 2]])
            t = W("scalar", lambda a, b, par=par, q=q, src=small[turn % 2]: a.activation(
                hh[:, par, q:q + 4, :].rearrange("p q d -> p (q d)"), src[:, :], ACT.Copy), [t])
            small_free[turn % 2] = t
            got_h.append(t)
            turn += 1
    t = W("vector", lambda v, b: v.tensor_copy(
        bv_cols[:, :, :], xb[:, 2, :].unsqueeze(2).to_broadcast([DX, NX, T2])), [got_xb])

    def value_bias(pe, b, dst=big[lot % 3]):
        for h in range(NX):
            r0 = (h % 2) * T2
            last = pe.matmul(dst[r0:r0 + T2, (h // 2) * D:(h // 2 + 1) * D], bv_cols[:, h, :],
                             xw["xo"][:, h, :], start=True, stop=True)
        return last
    t = W("tensor", value_bias, [t, got_xo, big_free[lot % 3]])
    got_ub = W("vector", lambda v, b, src=big[lot % 3]: v.tensor_copy(u_bias[:, :], src[:, :]), [t])
    big_free[lot % 3] = got_ub
    lot += 1

    for b0 in range(NB):
        half, buf = b0 // (NB // 2), stage_buf[b0 // (NB // 2)]

        def value_side(pe, b, b0=b0, dst=big[lot % 3]):
            for k in range(2):
                for par in range(2):
                    last = pe.matmul(dst[par * T2:(par + 1) * T2, k * 512:(k + 1) * 512],
                                     ctx[:, b0 * T2:(b0 + 1) * T2],
                                     hh[:, par, 4 * k:4 * k + 4, :].rearrange("p q d -> p (q d)"),
                                     start=True, stop=True)
            return last
        t = W("tensor", value_side, [*got_h, got_ctx, big_free[lot % 3]])
        t = W("vector", lambda v, b, b0=b0, buf=buf, src=big[lot % 3]: v.tensor_tensor(
            buf[:, b0 % (NB // 2), :], src[:, :], u_bias[:, :], ALU.add), [t, stored[half], got_ub])
        big_free[lot % 3] = t
        lot += 1
        if b0 % (NB // 2) == NB // 2 - 1:
            plan.dma("sync", "W", "u_out", lambda e, b, half=half, buf=buf: e.dma_start(
                g["u_all"][half * NB // 2:(half + 1) * NB // 2].rearrange("b p n -> p b n"), buf[:, :, :]), [t])

    def part(hi, lo, raw, after):
        t = W("gpsimd", lambda e, b: e.tensor_copy(hi, raw), after)
        return W("vector", lambda v, b: v.tensor_tensor(lo, raw, f32(hi), ALU.subtract), [t])
    part(g["wqk_hi"][:, :, :], g["wqk_lo"][:, :, :], wqk_raw[:, :, :], [got_wqk])
    for e0 in range(NE):
        if e0 == NE // 2:
            got_w1 = plan.dma("sync", "W", "w1_b", lambda e, b: e.dma_start(
                w1_raw[:, :, :], g["w1"][:, NE // 2:, :]), [t])
        t = part(w1_hi[:, e0, :], w1_lo[:, e0, :], w1_raw[:, e0 % (NE // 2), :], [got_w1])
    plan.finish()

    sems = {n: nc.alloc_semaphore(n + "_w") for n in plan.counts}
    with nc.Block() as block:
        for name in ("sync", "gpsimd", "vector", "scalar", "tensor"):
            def body(eng, name=name):
                plan.emit(eng, queues.get(name, []), sems, 0, False)
                if name == "sync":
                    for s in ("dma_r_out", "dma_a_out0", "dma_a_out1", "dma_u_out", "dma_rest"):
                        eng.wait_ge(sems[s], plan.per_batch[s])
            getattr_free = {"sync": block.sync, "gpsimd": block.gpsimd, "vector": block.vector,
                            "scalar": block.scalar, "tensor": block.tensor}
            getattr_free[name](body)


def main(nc, stack, sb, big, small, g):
    ident, minus_half = g["ident"], g["minus_half"]

    x_in = sb("x_in", [P, ST, D])
    x_keep = sb("x_keep", [P, ST, D])
    xn = sb("xn", [P, ST, D])
    stats_a, moments_a, rstd_a = sb("stats_a", [P, ST, 6]), sb("moments_a", [P, ST, 2]), sb("rstd_a", [P, ST])
    xt, xt_hi, xt_lo = sb("xt", [P, S]), sb("xt_hi", [P, S], F32R), sb("xt_lo", [P, S], F32R)
    parts = sb("parts", [P, NPIECE, 2, S], BF16)
    rest = sb("rest", [P, 2 * S])
    v_cols = sb("v_cols", [P, ST, NH, 32])
    q_stack = sb("q_stack", [P, NH, S], BF16)
    k_stack = sb("k_stack", [P, NH, S], BF16)
    max_a = sb("max_a", [P, ST, NH])
    max_parts = sb("max_parts", [NH, NPIECE, S], BF16)
    max_rest = sb("max_rest", [NH, S])
    NPROB = 3
    probs = [sb(f"probs{n}", [P, 4, S]) for n in range(NPROB)]
    o_cols = sb("o_cols", [P, 4, S])
    rec_a = sb("rec_a", [P, ST, NH])
    attn = sb("attn", [P, ST, NH, DK])
    attn_t = sb("attn_t", [P, S])
    x2, x2_bo, xn2, x2t = sb("x2", [P, ST, D]), sb("x2_bo", [P, ST, D]), sb("xn2", [P, ST, D]), sb("x2t", [P, S])
    stats_b, moments_b, rstd_b = sb("stats_b", [P, ST, 6]), sb("moments_b", [P, ST, 2]), sb("rstd_b", [P, ST])
    a_b, u_b = sb("a_b", [P, NX * T2]), sb("u_b", [P, NPAIR, D])
    r_b = sb("r_b", [NPIECE, NX * T2], BF16)
    mask_i = sb("mask_i", [P, ST, T2], I32)
    mask_neg = sb("mask_neg", [P, ST, T2])
    any_b = sb("any_b", [P, ST])
    s_b = sb("s_b", [P, ST, NX, T2])
    max_b, rec_b = sb("max_b", [P, ST, NX]), sb("rec_b", [P, ST, NX])
    p_t = sb("p_t", [P, NPAIR, S])
    x3, xn3, x3t = sb("x3", [P, ST, D]), sb("xn3", [P, ST, D]), sb("x3t", [P, S])
    x3_hi, x3_lo = sb("x3_hi", [P, S], F32R), sb("x3_lo", [P, S], F32R)
    logits, top_v = sb("logits", [P, ST, NE]), sb("top_v", [P, ST, NE])
    top_i, top_if = sb("top_i", [P, ST, NE], U32), sb("top_if", [P, ST, 2])
    gate = sb("gate", [P, 4, ST])
    cw2 = sb("cw2", [P, 2, ST, NE])
    cw = sb("cw", [P, ST, NE])
    cw_t = sb("cw_t", [NE, S])
    acc = sb("acc", [P, ST, D])
    hidden = [sb(f"hidden{n}", [P, FB, S]) for n in range(2)]

    plan = Plan()

    def iteration(has):
        plan.start()
        on_small = [0, [None, None]]
        if "B" in has or "C" in has:
            on_small[1] = [Done("vector_B", 0, END)] * 2

        def take_small():
            n = on_small[0] % 2
            on_small[0] += 1
            return n, small[n], on_small[1][n]

        def free_small(n, done):
            on_small[1][n] = done

        last_of = {}
        big2 = {"free": None}

        def stage_a():
            A = lambda engine, make, after=(): plan.step(engine, "A", make, after)
            before = lambda d: Done(d.sem, d.lead - 1, d.count)
            prev = lambda engine: Done(f"{engine}_A", 1, END)
            got_x = plan.dma("sync", "A", "x", lambda e, b: e.dma_start(
                x_in[:, :, :], g["x"][b].rearrange("(n p) d -> p n d", p=P)), [prev("vector"), prev("scalar")])
            t_n = layer_norm(plan, "A", x_in, xn, stats_a, moments_a, rstd_a, minus_half, [got_x], [])
            yield
            n, ps_t, free = take_small()
            t = transpose_tiles(plan, "A", ps_t, xn, ident, [t_n, free])
            t_xt = A("scalar", lambda a, b: a.activation(xt[:, :], ps_t[:, 0:S], ACT.Copy), [t])
            t_hi = A("vector", lambda v, b: v.tensor_copy(xt_hi[:, :], xt[:, :]), [t_xt])
            t_lo = A("vector", lambda v, b: v.tensor_tensor(xt_lo[:, :], xt[:, :], f32(xt_hi[:, :]),
                                                           ALU.subtract), [t_hi])
            free_small(n, t_xt)
            yield
            n, ps_qk, free = take_small()

            def project(pe, b):
                for c in range(2):
                    last = three_passes(pe, ps_qk[:, c * S:(c + 1) * S], g["wqk_hi"][:, c, :], g["wqk_lo"][:, c, :],
                                        xt_hi[:, :], xt_lo[:, :])
                return last
            t_qk = A("tensor", project, [t_lo, free])
            t = A("vector", lambda v, b: v.tensor_copy(
                parts[:, 0, :, :].rearrange("p c s -> p (c s)"), ps_qk[:, :]), [t_qk])
            t = A("vector", lambda v, b: v.tensor_tensor(
                rest[:, :], ps_qk[:, :], parts[:, 0, :, :].rearrange("p c s -> p (c s)"), ALU.subtract), [t])
            free_small(n, t)
            t = A("vector", lambda v, b: v.tensor_copy(
                parts[:, 1, :, :].rearrange("p c s -> p (c s)"), rest[:, :]), [t])
            t = A("vector", lambda v, b: v.tensor_tensor(
                parts[:, 2, :, :].rearrange("p c s -> p (c s)"), rest[:, :],
                parts[:, 1, :, :].rearrange("p c s -> p (c s)"), ALU.subtract), [t])
            for c in range(2):
                t_w = plan.dma("sync", "A", "parts_out", lambda e, b, c=c: e.dma_start(
                    g["parts_dram"][c].rearrange("k p s -> p k s"), parts[:, :, c, :]), [t])
            for a in range(NPIECE):
                t_st = plan.dma("sync", "A", "stacks", lambda e, b, a=a: e.dma_start(
                    q_stack[a * 24:(a + 1) * 24, :, :],
                    g["parts_dram"][0].rearrange("k (d h) s -> (k d) h s", d=DK)), [t_w, prev("tensor")])
                for k in range(NPIECE):
                    t_st = plan.dma("sync", "A", "stacks", lambda e, b, a=a, k=k: e.dma_start(
                        k_stack[a * 24 + k * 8:a * 24 + k * 8 + 8, :, :],
                        g["parts_dram"][1, a].rearrange("(d h) s -> d h s", d=DK)), [t_w, prev("tensor")])
            n, ps_v, free = take_small()

            def values(pe, b):
                for m in range(ST):
                    last = pe.matmul(ps_v[:, m * P:(m + 1) * P], xt[:, m * P:(m + 1) * P], g["wv_wo"][:, 0, :],
                                     start=True, stop=True)
                return last
            t = A("tensor", values, [t_xt, free])
            t_v = A("scalar", lambda a, b: a.activation(
                v_cols[:, :, :, 0:DK], ps_v[:, 0:ST * P].rearrange("p (m h d) -> p m h d", m=ST, h=NH),
                ACT.Copy), [t, prev("tensor")])
            free_small(n, t_v)
            yield
            for m in range(ST):
                for h0 in range(0, NH, 4):
                    def scores(pe, b, m=m, h0=h0):
                        for h in range(h0, h0 + 4):
                            last = pe.matmul(big[2][:, (h - h0) * S:(h - h0 + 1) * S],
                                             q_stack[0:ROWS, h, m * P:(m + 1) * P], k_stack[0:ROWS, h, :],
                                             start=True, stop=True)
                        return last
                    t = A("tensor", scores, [t_st, big2["free"]])
                    t_mx = big2["free"] = A("vector", lambda v, b, m=m, h0=h0: v.tensor_reduce(
                        max_a[:, m, h0:h0 + 4], big[2][:, :].rearrange("p (h t) -> p h t", h=4),
                        AX.X, ALU.max), [t])
                    yield
            n, ps_m, free = take_small()

            def turn_max(pe, b):
                for m in range(ST):
                    last = pe.transpose(ps_m[0:NH, m * P:(m + 1) * P], max_a[:, m, :], ident[:, :])
                return last
            t = A("tensor", turn_max, [t_mx, free])
            t = A("vector", lambda v, b: v.tensor_scalar(
                max_parts[:, 0, :], ps_m[0:NH, 0:S], -1.0, None, ALU.mult), [t])
            t = A("vector", lambda v, b: v.scalar_tensor_tensor(
                max_rest[:, :], ps_m[0:NH, 0:S], -1.0, max_parts[:, 0, :], ALU.mult, ALU.subtract), [t])
            free_small(n, t)
            t = A("vector", lambda v, b: v.tensor_copy(max_parts[:, 1, :], max_rest[:, :]), [t])
            t = A("vector", lambda v, b: v.tensor_tensor(
                max_parts[:, 2, :], max_rest[:, :], max_parts[:, 1, :], ALU.subtract), [t])
            for k in range(NPIECE):
                t_m = plan.dma("sync", "A", "max_rows", lambda e, b, k=k: e.dma_start(
                    q_stack[ROWS + k:ROWS + k + 1, :, :], max_parts[:, k, :]), [t])
            A("scalar", lambda a, b: a.activation(x_keep[:, :, :], x_in[:, :, :], ACT.Copy),
              [got_x, last_of.get("x2")])
            yield
            t_exp, t_s = [None] * 8, [None] * 8
            t_pv = [None] * 8
            big_free = [None, None]

            def by_key(u):
                h0, m = 4 * (u // ST), u % ST
                ps = big[u % 2]

                def make(pe, b):
                    for h in range(h0, h0 + 4):
                        last = pe.matmul(ps[:, (h - h0) * S:(h - h0 + 1) * S],
                                         k_stack[0:ROWS + NPIECE, h, m * P:(m + 1) * P],
                                         q_stack[0:ROWS + NPIECE, h, :], start=True, stop=True)
                    return last
                t_s[u] = A("tensor", make, [t_m, big_free[u % 2]])
                t_exp[u] = A("scalar", lambda a, b: a.activation(
                    probs[u % NPROB][:, :, :].rearrange("p h s -> p (h s)"), ps[:, :], ACT.Exp, scale=SCALE_A),
                    [t_s[u], t_pv[u - NPROB] if u >= NPROB else None])
                big_free[u % 2] = t_exp[u]

            def times_v(u):
                h0, m = 4 * (u // ST), u % ST

                def make(pe, b):
                    for h in range(h0, h0 + 4):
                        j = h - h0
                        last = pe.matmul(big[2][32 * j:32 * j + 32, (h0 // 4) * S:(h0 // 4 + 1) * S],
                                         v_cols[:, m, h, :], probs[u % NPROB][:, j, :],
                                         start=(m == 0), stop=(m == ST - 1))
                    return last
                t_pv[u] = A("tensor", make, [t_exp[u], t_v])

            by_key(0)
            by_key(1)
            for u in range(8):
                times_v(u)
                if u + 2 < 8:
                    by_key(u + 2)
                yield

        def stage_b():
            B = lambda engine, make, after=(): plan.step(engine, "B", make, after)
            prev = lambda engine: Done(f"{engine}_B", 0, END)
            free = [prev("tensor"), prev("vector")]
            plan.dma("sync", "B", "b_in", lambda e, b: e.dma_start(a_b[:, :], g["a_all"][b]), free)
            plan.dma("sync", "B", "b_in", lambda e, b: e.dma_start(
                u_b[:, :, :], g["u_all"][b].rearrange("p (q d) -> p q d", d=D)), free)
            plan.dma("sync", "B", "b_in", lambda e, b: e.dma_start(
                r_b[:, :].rearrange("k (h t) -> k h t", t=T2), g["r_all"][:, b]), free)
            got_b = plan.dma("sync", "B", "b_in", lambda e, b: e.dma_start(
                mask_i[:, :, :], g["mask"][b].rearrange("(n p) t -> p n t", p=P)), free)
            t = B("scalar", lambda a, b: a.activation(
                o_cols[:, :, :].rearrange("p q s -> p (q s)"), big[2][:, :], ACT.Copy), [Done("tensor_A", 1, END)])
            big2["free"] = t
            yield
            for m in range(ST):
                n, ps, free = take_small()

                def turn(pe, b, ps=ps, m=m):
                    for q in range(4):
                        last = pe.transpose(ps[:, q * P:(q + 1) * P], o_cols[:, q, m * P:(m + 1) * P], ident[:, :])
                    return last
                t1 = B("tensor", turn, [t, free])
                cols = ps[:, :].rearrange("p (h w) -> p h w", w=32)
                t2 = B("vector", lambda v, b, m=m, cols=cols: v.reciprocal(rec_a[:, m, :], cols[:, :, DK]), [t1])
                t_at = B("vector", lambda v, b, m=m, cols=cols: v.tensor_tensor(
                    attn[:, m, :, :], cols[:, :, 0:DK], rec_a[:, m, :].unsqueeze(2).to_broadcast([P, NH, DK]),
                    ALU.mult), [t2])
                free_small(n, t_at)
            yield
            n, ps1, free = take_small()
            t = transpose_tiles(plan, "B", ps1, attn[:, :, :, :].rearrange("p m h d -> p m (h d)"), ident,
                                [t_at, free])
            t = B("scalar", lambda a, b: a.activation(attn_t[:, :], ps1[:, 0:S], ACT.Copy), [t])
            free_small(n, t)
            yield
            n, ps2, free = take_small()

            def project(pe, b):
                for m in range(ST):
                    last = pe.matmul(ps2[:, m * P:(m + 1) * P], attn_t[:, m * P:(m + 1) * P], g["wv_wo"][:, 1, :],
                                     start=True, stop=True)
                return last
            t = B("tensor", project, [t, free])
            t = last_of["x2"] = B("vector", lambda v, b: v.tensor_tensor(
                x2[:, :, :], ps2[:, 0:S].rearrange("p (m d) -> p m d", m=ST), x_keep[:, :, :], ALU.add),
                [t, Done("scalar_A", 1, END)])
            free_small(n, t)
            t_bo = B("gpsimd", lambda e, b: e.tensor_tensor(
                x2_bo[:, :, :], x2[:, :, :], g["bo_all"][:, :].unsqueeze(1).to_broadcast([P, ST, D]), ALU.add), [t])
            t_n = layer_norm(plan, "B", x2, xn2, stats_b, moments_b, rstd_b, minus_half, [t], [])
            t_mk = B("vector", lambda v, b: v.tensor_scalar(
                mask_neg[:, :, :], mask_i[:, :, :], 0.0, MASKED / SCALE_B, ALU.is_equal, ALU.mult), [got_b])
            t = B("vector", lambda v, b: v.tensor_reduce(any_b[:, :], mask_neg[:, :, :], AX.X, ALU.max), [t_mk])
            t_any = B("vector", lambda v, b: v.tensor_scalar(
                any_b[:, :], any_b[:, :], 0.0, None, ALU.is_equal), [t])
            yield
            n, ps3, free = take_small()
            t = transpose_tiles(plan, "B", ps3, xn2, ident, [t_n, free])
            t_xt = B("scalar", lambda a, b: a.activation(x2t[:, :], ps3[:, 0:S], ACT.Copy), [t])
            free_small(n, t_xt)
            yield
            t_sub = [None] * ST
            for m in range(ST):
                def scores(pe, b, m=m):
                    for k in range(2):
                        cols = slice(k * 512, (k + 1) * 512)
                        pe.matmul(big[2][:, cols], x2t[:, m * P:(m + 1) * P], a_b[:, cols], start=True, stop=False)
                        last = pe.matmul(big[2][:, cols], g["ones_row"][:, :], r_b[:, cols],
                                         start=False, stop=True)
                    return last
                t = B("tensor", scores, [t_xt, got_b, big2["free"]])
                t = big2["free"] = B("vector", lambda v, b, m=m: v.tensor_tensor(
                    s_b[:, m, :, :], big[2][:, :].rearrange("p (h t) -> p h t", h=NX),
                    mask_neg[:, m, :].unsqueeze(1).to_broadcast([P, NX, T2]), ALU.add), [t, t_mk])
                t = B("vector", lambda v, b, m=m: v.tensor_reduce(
                    max_b[:, m, :], s_b[:, m, :, :], AX.X, ALU.max), [t])
                t_sub[m] = B("gpsimd", lambda e, b, m=m: e.tensor_tensor(
                    s_b[:, m, :, :], s_b[:, m, :, :], max_b[:, m, :].unsqueeze(2).to_broadcast([P, NX, T2]),
                    ALU.subtract), [t])
                yield
            t_p = [None] * ST
            for m in range(ST):
                t = B("scalar", lambda a, b, m=m: a.activation(
                    s_b[:, m, :, :], s_b[:, m, :, :], ACT.Exp, scale=SCALE_B), [t_sub[m]])
                t = B("vector", lambda v, b, m=m: v.tensor_reduce(
                    rec_b[:, m, :], s_b[:, m, :, :], AX.X, ALU.add), [t])
                t = B("vector", lambda v, b, m=m: v.reciprocal(rec_b[:, m, :], rec_b[:, m, :]), [t])
                t = B("vector", lambda v, b, m=m: v.tensor_scalar(
                    rec_b[:, m, :], rec_b[:, m, :], any_b[:, m:m + 1], None, ALU.mult), [t, t_any])
                t_p[m] = B("vector", lambda v, b, m=m: v.tensor_tensor(
                    s_b[:, m, :, :], s_b[:, m, :, :], rec_b[:, m, :].unsqueeze(2).to_broadcast([P, NX, T2]),
                    ALU.mult), [t])
            yield
            t_pt = []
            for m in range(ST):
                for q0 in range(0, NPAIR, 4):
                    n, ps, free = take_small()

                    def turn(pe, b, ps=ps, m=m, q0=q0):
                        for q in range(4):
                            last = pe.transpose(
                                ps[:, q * P:(q + 1) * P],
                                s_b[:, m, 2 * (q0 + q):2 * (q0 + q) + 2, :].rearrange("p h t -> p (h t)"), ident[:, :])
                        return last
                    t = B("tensor", turn, [t_p[m], free])
                    to = p_t[:, q0:q0 + 4, m * P:(m + 1) * P]
                    src = ps[:, :].rearrange("p (q s) -> p q s", q=4)
                    t = B("vector", lambda v, b, to=to, src=src: v.tensor_copy(to, src), [t])
                    free_small(n, t)
                    t_pt.append(t)
                yield
            n, ps4, free = take_small()

            def times_u(pe, b):
                for m in range(ST):
                    for q in range(NPAIR):
                        last = pe.matmul(ps4[:, m * P:(m + 1) * P], p_t[:, q, m * P:(m + 1) * P], u_b[:, q, :],
                                         start=(q == 0), stop=(q == NPAIR - 1))
                return last
            t = B("tensor", times_u, [*t_pt, got_b, free])
            t_x3 = B("vector", lambda v, b: v.tensor_tensor(
                x3[:, :, :], ps4[:, 0:S].rearrange("p (m d) -> p m d", m=ST), x2_bo[:, :, :], ALU.add), [t, t_bo])
            free_small(n, t_x3)
            t_n = layer_norm(plan, "B", x3, xn3, stats_b, moments_b, rstd_b, minus_half, [t_x3], [])
            yield
            n, ps5, free = take_small()
            t = transpose_tiles(plan, "B", ps5, xn3, ident, [t_n, free])
            t_xt = B("scalar", lambda a, b: a.activation(x3t[:, :], ps5[:, 0:S], ACT.Copy), [t])
            free_small(n, t_xt)
            t = B("vector", lambda v, b: v.tensor_copy(x3_hi[:, :], x3t[:, :]), [t_xt, last_of.get("up")])
            B("vector", lambda v, b: v.tensor_tensor(
                x3_lo[:, :], x3t[:, :], f32(x3_hi[:, :]), ALU.subtract), [t])
            yield
            n, ps6, free = take_small()

            def route(pe, b):
                for m in range(ST):
                    last = pe.matmul(ps6[:, m * NE:(m + 1) * NE], x3t[:, m * P:(m + 1) * P], g["wr"][:, :],
                                     start=True, stop=True)
                return last
            t = B("tensor", route, [t_xt, free])
            t = B("vector", lambda v, b: v.tensor_copy(
                logits[:, :, :].rearrange("p m e -> p (m e)"), ps6[:, 0:ST * NE]), [t])
            free_small(n, t)

            def largest(v, b):
                for m in range(ST):
                    last = v.max(top_v[:, m, :], logits[:, m, :])
                return last

            def places(v, b):
                for m in range(ST):
                    last = v.max_index(top_i[:, m, :], top_v[:, m, :], logits[:, m, :])
                return last
            t = plan.step("vector", "B", largest, [t], apart=True)
            t_i = plan.step("vector", "B", places, [t], apart=True)
            t = B("vector", lambda v, b: v.tensor_tensor(
                gate[:, 0, :], top_v[:, :, 1], top_v[:, :, 0], ALU.subtract), [t])
            t_e = B("gpsimd", lambda e, b: e.tensor_tensor(
                gate[:, 1, :], g["euler"][:, :], gate[:, 0, :], ALU.pow), [t])
            t_if = B("vector", lambda v, b: v.tensor_copy(top_if[:, :, :], top_i[:, :, 0:2]), [t_i])
            t = B("vector", lambda v, b: v.tensor_scalar(gate[:, 2, :], gate[:, 1, :], 1.0, None, ALU.add), [t_e])
            t = B("vector", lambda v, b: v.reciprocal(gate[:, 2, :], gate[:, 2, :]), [t])
            t = B("vector", lambda v, b: v.tensor_tensor(
                gate[:, 3, :], gate[:, 1, :], gate[:, 2, :], ALU.mult), [t])

            def weigh(v, b):
                for k in range(2):
                    for m in range(ST):
                        last = v.tensor_scalar(cw2[:, k, m, :], g["iota8"][:, :], top_if[:, m, k:k + 1],
                                               gate[:, 2 + k, m:m + 1], ALU.is_equal, ALU.mult)
                return last
            t = B("vector", weigh, [t, t_if])
            t_cw = B("vector", lambda v, b: v.tensor_tensor(
                cw[:, :, :], cw2[:, 0, :, :], cw2[:, 1, :, :], ALU.add), [t, last_of.get("mix")])
            yield
            n, ps7, free = take_small()

            def turn_cw(pe, b):
                for m in range(ST):
                    last = pe.transpose(ps7[0:NE, m * P:(m + 1) * P], cw[:, m, :], ident[:, :])
                return last
            t = B("tensor", turn_cw, [t_cw, free])
            t = B("vector", lambda v, b: v.tensor_copy(cw_t[:, :], ps7[0:NE, 0:S]), [t])
            free_small(n, t)
            n, ps8, free = take_small()

            def bias2(pe, b):
                for m in range(ST):
                    last = pe.matmul(ps8[:, m * P:(m + 1) * P], cw_t[:, m * P:(m + 1) * P], g["b2_sb"][:, :],
                                     start=True, stop=True)
                return last
            t = B("tensor", bias2, [t, free])
            t = B("vector", lambda v, b: v.tensor_tensor(
                acc[:, :, :], ps8[:, 0:S].rearrange("p (m d) -> p m d", m=ST), x3[:, :, :], ALU.add),
                [t, last_of.get("stored")])
            free_small(n, t)
            yield

        def stage_c():
            C = lambda engine, make, after=(): plan.step(engine, "C", make, after)
            ready = Done("vector_B", 0, END)
            t_up, t_gelu, t_down = {}, {}, {}
            t_mix = [ready, ready]

            def up(e0):
                ps = big[e0 % 2]

                def make(pe, b):
                    for f in range(FB):
                        cols = slice(f * P, (f + 1) * P)
                        last = three_passes(pe, ps[:, f * S:(f + 1) * S], g["w1_hi"][:, e0, cols],
                                            g["w1_lo"][:, e0, cols], g_x3_hi, g_x3_lo)
                    return last
                g_x3_hi, g_x3_lo = x3_hi[:, :], x3_lo[:, :]
                t_up[e0] = last_of["up"] = C("tensor", make, [ready, t_gelu.get(e0 - 2)])

                def gelu(a, b):
                    for f in range(FB):
                        last = a.activation(hidden[e0 % 2][:, f, :], ps[:, f * S:(f + 1) * S], ACT.Gelu,
                                            bias=g["b1_sb"][:, e0 * FB + f:e0 * FB + f + 1])
                    return last
                t_gelu[e0] = C("scalar", gelu, [t_up[e0], t_down.get(e0 - 2)])

            def down(e0):
                n, ps, free = take_small()

                def make(pe, b):
                    for m in range(ST):
                        for f in range(FB):
                            last = pe.matmul(ps[:, m * P:(m + 1) * P], hidden[e0 % 2][:, f, m * P:(m + 1) * P],
                                             g["w2_sb"][:, e0, f, :], start=(f == 0), stop=(f == FB - 1))
                    return last
                t_down[e0] = C("tensor", make, [t_gelu[e0], free])
                for m in range(ST):
                    t_mix[m] = C("vector", lambda v, b, m=m: v.scalar_tensor_tensor(
                        acc[:, m, :], ps[:, m * P:(m + 1) * P], cw[:, m, e0:e0 + 1], acc[:, m, :],
                        ALU.mult, ALU.add), [t_down[e0], t_mix[m]])
                last_of["mix"] = t_mix[ST - 1]
                free_small(n, t_mix[ST - 1])

            up(0)
            yield
            for e0 in range(NE):
                if e0 + 1 < NE:
                    up(e0 + 1)
                    yield
                down(e0)
                yield
            last_of["stored"] = plan.dma("gpsimd", "C", "out", lambda e, b: e.dma_start(
                g["out"][b].rearrange("(n p) d -> p n d", p=P), acc[:, :, :]), t_mix)
            yield

        order = ("B A C A B C B C A B C C B C B"
                 " C B C C B C A"
                 " A C A C A C A C A C A C A C C A"
                 " B A B A A B A B A A B A B A A B A").split()
        running = {"A": stage_a(), "B": stage_b(), "C": stage_c()}
        for s in order:
            if s in has:
                next(running[s], None)
        for s in "CBA":
            if s in has:
                for _ in running[s]:
                    pass
        queues = plan.queues
        plan.finish()
        return queues

    segments = [(-2, iteration("A")), (-1, iteration("AB")), ("loop", iteration("ABC")),
                (NB - 2, iteration("BC")), (NB - 1, iteration("C"))]

    sems = {n: nc.alloc_semaphore(n) for n in plan.per_batch}
    ready = nc.alloc_semaphore("constants")

    with nc.Block() as block:
        def run(name):
            def body(eng):
                if name == "vector":
                    eng.memset(k_stack[64:96, :, :], 1.0).then_inc(ready, 1)
                    eng.memset(v_cols[:, :, :, :], 0.0).then_inc(ready, 1)
                    eng.wait_ge(ready, 2)
                    eng.memset(v_cols[:, :, :, DK:DK + 1], 1.0).then_inc(ready, 1)
                eng.wait_ge(ready, 3)
                for j, queues in segments:
                    queue = queues.get(name, [])
                    if not queue:
                        continue
                    if j == "loop":
                        with eng.Fori(0, NB - 2) as reg:
                            plan.emit(eng, queue, sems, reg, True, g["spare"][:, :])
                    else:
                        plan.emit(eng, queue, sems, j, False)
                if name == "gpsimd":
                    eng.wait_ge(sems["dma_out"], NB * plan.per_batch["dma_out"])
            return body
        block.sync(run("sync"))
        block.gpsimd(run("gpsimd"))
        block.vector(run("vector"))
        block.scalar(run("scalar"))
        block.tensor(run("tensor"))


def kernel(x, ctx_1024, mask_BxSxS2_ik1, L0_attn_W_q, L0_attn_W_k, L0_attn_W_v, L0_attn_W_out, L0_xattn_Wq,
           L0_xattn_bq, L0_xattn_Wk, L0_xattn_bk, L0_xattn_Wv, L0_xattn_bv, L0_xattn_Wo, L0_xattn_bo,
           L0_ffn_w_router, L0_ffn_w1, L0_ffn_b1, L0_ffn_w2, L0_ffn_b2):
    import concourse.bacc as bacc
    from concourse.bass_utils import run_bass_kernel_spmd

    A = np.asarray
    by_head = lambda w: A(w).reshape(NX, DX, D).transpose(1, 0, 2)
    turned = lambda w: A(w).reshape(NH, DK, D).transpose(2, 1, 0).reshape(D, P)
    arrays = {
        "x": A(x),
        "ctx_t": A(ctx_1024).reshape(NB * T2, D).T,
        "mask": A(mask_BxSxS2_ik1),
        "attn_w": np.stack([turned(L0_attn_W_q), turned(L0_attn_W_k), A(L0_attn_W_v).T, A(L0_attn_W_out).T], 1),
        "xq": by_head(L0_xattn_Wq),
        "xk": by_head(L0_xattn_Wk),
        "xv": by_head(L0_xattn_Wv),
        "xo": A(L0_xattn_Wo).reshape(D, NX, DX).transpose(2, 1, 0),
        "xbias": np.stack([A(v).reshape(NX, DX).T for v in (L0_xattn_bq, L0_xattn_bk, L0_xattn_bv)], 1),
        "bo": A(L0_xattn_bo),
        "w_router": A(L0_ffn_w_router).T,
        "w1": A(L0_ffn_w1).transpose(2, 0, 1),
        "b1": A(L0_ffn_b1).reshape(NE * FB, P).T,
        "w2": A(L0_ffn_w2).reshape(NE, D, FB, P).transpose(3, 0, 2, 1),
        "b2": A(L0_ffn_b2),
    }
    arrays = {n: np.ascontiguousarray(a) for n, a in arrays.items()}
    nc = bacc.Bacc("TRN2", target_bir_lowering=False, num_devices=1)
    aps = {n: nc.dram_tensor(n, a.shape, mybir.dt.from_np(a.dtype), kind="ExternalInput").ap()
           for n, a in arrays.items()}
    out = nc.dram_tensor("out", (NB, S, D), F32, kind="ExternalOutput").ap()
    build(nc, *aps.values(), out)
    r = run_bass_kernel_spmd(nc, [arrays], core_ids=[0])
    return r.results[0]["out"]
```

```python
from contextlib import ExitStack

import concourse.bass as bass
import concourse.mybir as mybir
import numpy as np

F32, F32R, BF16 = mybir.dt.float32, mybir.dt.float32r, mybir.dt.bfloat16
I32, U32 = mybir.dt.int32, mybir.dt.uint32
ALU, ACT, AX = mybir.AluOpType, mybir.ActivationFunctionType, mybir.AxisListType

P = 128
NB, S, D = 16, 256, 128
ST = S // P
NH, DK = 16, 8
T2, DX = 64, 64
NX = 16
NPAIR = NX // 2
NE, FF = 8, 512
FB = FF // P
NPIECE = 3
ROWS = NPIECE * NPIECE * DK
EPS = 1e-5
MASKED = -1e20
SCALE_A, SCALE_B = DK ** -0.5, DX ** -0.5
END = "end"

ORDER = [x.split(":") for x in (
    "A:norm B:sums C:up0 B:normalise C:route C:up1 A:turn B:turn C:down0 A:qkv C:up2 B:project "
    "C:down1 C:up3 B:turn x2 C:down2 B:scores0 C:up4 A:max0 C:down3 B:scores1 A:max1 C:up5 A:max2 C:down4 "
    "A:max3 A:max4 C:up6 A:max5 C:down5 A:max6 C:up7 A:max7 C:down6 A:turn max B:exp C:down7 C:end "
    "A:values0 B:turn p0 A:values1 B:turn p1 A:values2 A:values3 B:times u A:values4 A:values5 "
    "A:values6 B:turn x3 A:values7 A:end B:end").replace("turn x", "turn_x").replace("turn m", "turn_m")
    .replace("turn p", "turn_p").replace("times u", "times_u").split()]
ORDER = [(stage, until.replace("_", " ")) for stage, until in ORDER]


class Done:

    def __init__(self, sem, lead, count):
        self.sem, self.lead, self.count = sem, lead, count


class Plan:

    LEAD = {"A": 2, "B": 1, "C": 0, "W": 0}

    def __init__(self):
        self.per_batch, self.points = {}, {}
        self.start()

    def start(self):
        self.counts, self.queues = {}, {}
        return self.queues

    def name(self, point, done):
        self.points[point] = done
        return done

    def before(self, point):
        d = self.points.get(point)
        return d and Done(d.sem, d.lead - 1, d.count)

    def finish(self):
        for sem, n in self.counts.items():
            assert self.per_batch.setdefault(sem, n) == n, sem

    def step(self, engine, stage, make, after=(), sem=None, add=1, apart=False):
        sem = sem or f"{engine}_{stage}"
        self.counts[sem] = self.counts.get(sem, 0) + add
        self.queues.setdefault(engine, []).append((list(after), make, sem, add, self.LEAD[stage], apart))
        return Done(sem, self.LEAD[stage], self.counts[sem])

    def dma(self, engine, stage, name, make, after=()):
        return self.step(engine, stage, make, after, f"dma_{name}", 16)

    def emit(self, eng, queue, sems, j, looped, spare=None):
        passed = {}
        for after, make, sem, add, lead, apart in queue:
            waits = 0
            for d in after:
                if d is None or (not looped and j + d.lead < 0):
                    continue
                k = self.per_batch[d.sem]
                count = k if d.count == END else d.count
                if passed.get((d.sem, d.lead), 0) >= count:
                    continue
                passed[d.sem, d.lead] = count
                eng.wait_ge(sems[d.sem], j * k + (d.lead * k + count))
                waits += 1
            if apart and looped and waits:
                eng.memset(spare, 0.0)
            make(eng, j + lead).then_inc(sems[sem], add)


def layer_norm(plan, stage, x, out, stats, moments, rstd, half, after, free):
    def statistics(v, b):
        for n in range(ST):
            last = v.bn_stats(stats[:, n, :], x[:, n, :])
        return last

    def aggregate(v, b):
        for n in range(ST):
            last = v.bn_aggr(moments[:, n, :], stats[:, n, :])
        return last

    def normalise(v, b):
        for n in range(ST):
            last = v.tensor_scalar(out[:, n, :], x[:, n, :], moments[:, n, 0:1], rstd[:, n:n + 1],
                                   ALU.subtract, ALU.mult)
        return last

    t = plan.step("vector", stage, statistics, after)
    t = plan.step("vector", stage, aggregate, [t], apart=True)
    t = plan.step("vector", stage, lambda v, b: v.tensor_scalar(
        rstd[:, :], moments[:, :, 1], EPS, None, ALU.add), [t])
    t = plan.step("gpsimd", stage, lambda g, b: g.tensor_tensor(
        rstd[:, :], rstd[:, :], half[:, :], ALU.pow), [t])
    return plan.step("vector", stage, normalise, [t, *free])


def transpose_tiles(plan, stage, dst, src, ident, after):
    def make(pe, b):
        for n in range(ST):
            last = pe.transpose(dst[:, n * P:(n + 1) * P], src[:, n, :], ident[:, :])
        return last
    return plan.step("tensor", stage, make, after)


def three_passes(pe, out, w_hi, w_lo, x_hi, x_lo, stop=True):
    pe.matmul(out, w_hi, x_hi, start=True, stop=False)
    pe.matmul(out, w_hi, x_lo, start=False, stop=False)
    return pe.matmul(out, w_lo, x_hi, start=False, stop=stop)


def f32(ap):
    return ap.bitcast(F32)


def build(nc, x, ctx_t, mask, attn_w, xq, xk, xv, xo, xbias, bo, w_router, w1, b1, w2, b2, out):
    stack = ExitStack()
    with stack:
        def sb(name, shape, dt=F32, at=stack):
            return at.enter_context(nc.sbuf_tensor(name, shape, dt))

        def psum(name, shape):
            return stack.enter_context(nc.psum_tensor(name, shape, F32))

        def dram(name, shape, dt):
            return nc.dram_tensor(name, shape, dt, kind="Internal").ap()

        a_all = dram("a_all", [NB, P, NX * T2], F32)
        u_all = dram("u_all", [NB, P, NPAIR * D], F32)
        r_all = dram("r_all", [NPIECE, NB, NX, T2], BF16)
        parts_dram = dram("parts_dram", [2, NPIECE, P, S], BF16)

        big = [psum(f"big{n}", [P, 2 * 512]) for n in range(3)]
        small = [psum(f"small{n}", [P, 512]) for n in range(2)]

        ident = sb("ident", [P, P])
        minus_half = sb("minus_half", [P, ST])
        euler = sb("euler", [P, ST])
        spare = sb("spare", [1, 1])
        iota8 = sb("iota8", [P, NE])
        iota_i = sb("iota_i", [P, NE], I32)
        ones_row = sb("ones_row", [NPIECE, P], BF16)
        wqk_hi = sb("wqk_hi", [P, 2, P], F32R)
        wqk_lo = sb("wqk_lo", [P, 2, P], F32R)
        wv_wo = sb("wv_wo", [P, 2, P])
        bo_all = sb("bo_all", [P, D])
        wr = sb("wr", [P, NE])
        w1_hi = sb("w1_hi", [P, NE, FF], F32R)
        w1_lo = sb("w1_lo", [P, NE, FF], F32R)
        w2_sb = sb("w2_sb", [P, NE, FB, D])
        b1_sb = sb("b1_sb", [P, NE * FB])
        b2_sb = sb("b2_sb", [NE, D])

        with ExitStack() as temporary:
            once(nc, temporary, sb, big, small, locals())

        main(nc, stack, sb, big, small, locals())


def once(nc, temporary, sb_, big, small, g):
    def sb(name, shape, dt=F32):
        return sb_(name, shape, dt, temporary)

    ident, w1_hi, w1_lo = g["ident"], g["w1_hi"], g["w1_lo"]
    wqk_raw = sb("wqk_raw", [P, 2, P])
    w1_raw = sb("w1_raw", [P, NE // 2, FF])
    ctx = sb("ctx", [P, NB * T2])
    xw = {n: sb(f"{n}_sb", [DX, NX, D]) for n in ("xq", "xk", "xv", "xo")}
    xb = sb("xb_sb", [DX, 3, NX])
    bv_cols = sb("bv_cols", [DX, NX, T2])
    bqk = sb("bqk", [DX, NX])
    ones_col = sb("ones_col", [DX, 1])
    gt = sb("gt", [P, NX, D])
    hh = sb("hh", [P, 2, NPAIR, D])
    vecs = sb("vecs", [P, 2, NX])
    beta = sb("beta", [NX, 1])
    u_bias = sb("u_bias", [P, NPAIR * D])
    r_f = sb("r_f", [NX, NB * T2])
    r_rest = sb("r_rest", [NX, NB * T2])
    r_parts = sb("r_parts", [NX, NPIECE, NB * T2], BF16)
    stage_buf = [sb(f"stage_buf{n}", [P, NB // 2, 1024]) for n in range(2)]

    plan = Plan()
    queues = plan.start()

    def load(name, dst, src, engine="sync"):
        return plan.dma(engine, "W", name, lambda e, b: e.dma_start(dst, src))

    W = lambda engine, make, after=(): plan.step(engine, "W", make, after)

    got_xk = load("xk", xw["xk"][:, :, :], g["xk"])
    got_xq = load("xq", xw["xq"][:, :, :], g["xq"])
    got_ctx = load("ctx", ctx[:, :], g["ctx_t"])
    got_xb = load("xbias", xb[:, :, :], g["xbias"])
    got_xv = load("xv", xw["xv"][:, :, :], g["xv"])
    got_xo = load("xo", xw["xo"][:, :, :], g["xo"])
    got_wqk = load("wqk", wqk_raw[:, :, :], g["attn_w"][:, 0:2, :])
    load("rest", g["wv_wo"][:, :, :], g["attn_w"][:, 2:4, :])
    load("rest", g["bo_all"][:, :], g["bo"].partition_broadcast(P))
    load("rest", g["wr"][:, :], g["w_router"])
    load("rest", g["b1_sb"][:, :], g["b1"])
    load("rest", g["b2_sb"][:, :], g["b2"])
    got_w1 = load("w1", w1_raw[:, :, :], g["w1"][:, 0:NE // 2, :])
    got_rest = load("rest", g["w2_sb"][:, :, :, :], g["w2"])

    t = W("gpsimd", lambda e, b: e.memset(ident[:, :], 0.0))
    got_ident = W("gpsimd", lambda e, b: e.affine_select(
        out=ident[:, :], in_=ident[:, :], compare_op=ALU.not_equal, fill=1.0, base=0,
        pattern=[[-1, P]], channel_multiplier=1), [t])
    t = W("gpsimd", lambda e, b: e.iota(g["iota_i"][:, :], pattern=[[1, NE]], base=0, channel_multiplier=0))
    W("vector", lambda e, b: e.tensor_copy(g["iota8"][:, :], g["iota_i"][:, :]), [t])
    W("vector", lambda e, b: e.memset(g["minus_half"][:, :], -0.5))
    W("vector", lambda e, b: e.memset(g["euler"][:, :], float(np.e)))
    W("vector", lambda e, b: e.memset(g["ones_row"][:, :], 1.0))
    got_ones = W("vector", lambda e, b: e.memset(ones_col[:, :], 1.0))

    small_free = [None, None]
    turn = 0
    got_g = []
    for h0 in range(0, NX, 4):
        def fold(pe, b, h0=h0, dst=small[turn % 2]):
            for h in range(h0, h0 + 4):
                last = pe.matmul(dst[:, (h - h0) * D:(h - h0 + 1) * D], xw["xk"][:, h, :], xw["xq"][:, h, :],
                                 start=True, stop=True)
            return last
        t = W("tensor", fold, [got_xk, got_xq, small_free[turn % 2]])
        t = W("vector", lambda v, b, h0=h0, src=small[turn % 2]: v.tensor_copy(
            gt[:, h0:h0 + 4, :].rearrange("p h d -> p (h d)"), src[:, :]), [t])
        small_free[turn % 2] = t
        got_g.append(t)
        turn += 1

    def vectors(pe, b, dst=small[turn % 2]):
        for h in range(NX):
            pe.matmul(dst[:, h:h + 1], xw["xq"][:, h, :], xb[:, 1, h:h + 1], start=True, stop=True)
            last = pe.matmul(dst[:, NX + h:NX + h + 1], xw["xk"][:, h, :], xb[:, 0, h:h + 1],
                             start=True, stop=True)
        return last
    t = W("tensor", vectors, [got_xb, small_free[turn % 2]])
    got_vecs = small_free[turn % 2] = W("vector", lambda v, b, src=small[turn % 2]: v.tensor_copy(
        vecs[:, :, :].rearrange("p a h -> p (a h)"), src[:, 0:2 * NX]), [t])
    turn += 1
    t = W("vector", lambda v, b: v.tensor_tensor(bqk[:, :], xb[:, 0, :], xb[:, 1, :], ALU.mult), [got_xb])
    t = W("tensor", lambda pe, b, dst=small[turn % 2]: pe.matmul(
        dst[0:NX, 0:1], bqk[:, :], ones_col[:, :], start=True, stop=True), [t, got_ones, small_free[turn % 2]])
    got_beta = small_free[turn % 2] = W("vector", lambda v, b, src=small[turn % 2]: v.tensor_copy(
        beta[:, :], src[0:NX, 0:1]), [t])
    turn += 1

    for half in range(2):
        cols = slice(half * 512, half * 512 + 512)
        t = W("tensor", lambda pe, b, dst=small[turn % 2], cols=cols: pe.matmul(
            dst[0:NX, :], vecs[:, 1, :], ctx[:, cols], start=True, stop=True),
            [got_vecs, got_ctx, small_free[turn % 2]])
        t = W("vector", lambda v, b, src=small[turn % 2], cols=cols: v.tensor_scalar(
            r_f[:, cols], src[0:NX, :], beta[:, 0:1], None, ALU.add), [t, got_beta])
        small_free[turn % 2] = t
        turn += 1
    t = W("vector", lambda v, b: v.tensor_copy(r_parts[:, 0, :], r_f[:, :]), [t])
    t = W("vector", lambda v, b: v.tensor_tensor(r_rest[:, :], r_f[:, :], r_parts[:, 0, :], ALU.subtract), [t])
    t = W("vector", lambda v, b: v.tensor_copy(r_parts[:, 1, :], r_rest[:, :]), [t])
    t = W("vector", lambda v, b: v.tensor_tensor(r_parts[:, 2, :], r_rest[:, :], r_parts[:, 1, :],
                                                 ALU.subtract), [t])
    for p in range(NPIECE):
        plan.dma("sync", "W", "r_out", lambda e, b, p=p: e.dma_start(
            g["r_all"][p].rearrange("b h t -> h b t"),
            r_parts[:, p, :].rearrange("h (b t) -> h b t", b=NB)), [t])

    big_free = [None, None, None]
    lot = 0
    stored = [None, None]
    for half in range(2):
        buf = stage_buf[half]
        for h in range(0, NX, 2):
            def key_side(pe, b, h=h, half=half, dst=big[lot % 3]):
                for k in range(2):
                    last = pe.matmul(dst[:, k * 512:(k + 1) * 512], gt[:, h + k, :],
                                     ctx[:, half * 512:(half + 1) * 512], start=True, stop=True)
                return last
            t = W("tensor", key_side, [*got_g, got_ctx, big_free[lot % 3]])

            def keep(e, k, h=h, buf=buf, src=big[lot % 3]):
                to = buf[:, :, (h + k) * T2:(h + k + 1) * T2]
                of = src[:, k * 512:(k + 1) * 512].rearrange("p (b t) -> p b t", t=T2)
                return to, of, vecs[:, 0, h + k:h + k + 1]
            t1 = W("scalar", lambda a, b, keep=keep: a.activation(
                keep(a, 0)[0], keep(a, 0)[1], ACT.Identity, bias=keep(a, 0)[2]), [t, got_vecs])
            t2 = W("vector", lambda v, b, keep=keep: v.tensor_scalar(
                keep(v, 1)[0], keep(v, 1)[1], keep(v, 1)[2], None, ALU.add), [t, got_vecs, t1])
            big_free[lot % 3] = t2
            lot += 1
        stored[half] = plan.dma("sync", "W", f"a_out{half}", lambda e, b, half=half, buf=buf: e.dma_start(
            g["a_all"][half * NB // 2:(half + 1) * NB // 2].rearrange("b p n -> p b n"), buf[:, :, :]), [t1, t2])

    got_h = []
    for par in range(2):
        for q in range(0, NPAIR, 4):
            def fold_v(pe, b, par=par, q=q, dst=small[turn % 2]):
                for k in range(4):
                    h = 2 * (q + k) + par
                    last = pe.matmul(dst[:, k * D:(k + 1) * D], xw["xv"][:, h, :], xw["xo"][:, h, :],
                                     start=True, stop=True)
                return last
            t = W("tensor", fold_v, [got_xv, got_xo, small_free[turn % 2]])
            t = W("scalar", lambda a, b, par=par, q=q, src=small[turn % 2]: a.activation(
                hh[:, par, q:q + 4, :].rearrange("p q d -> p (q d)"), src[:, :], ACT.Copy), [t])
            small_free[turn % 2] = t
            got_h.append(t)
            turn += 1
    t = W("vector", lambda v, b: v.tensor_copy(
        bv_cols[:, :, :], xb[:, 2, :].unsqueeze(2).to_broadcast([DX, NX, T2])), [got_xb])

    def value_bias(pe, b, dst=big[lot % 3]):
        for h in range(NX):
            r0 = (h % 2) * T2
            last = pe.matmul(dst[r0:r0 + T2, (h // 2) * D:(h // 2 + 1) * D], bv_cols[:, h, :],
                             xw["xo"][:, h, :], start=True, stop=True)
        return last
    t = W("tensor", value_bias, [t, got_xo, big_free[lot % 3]])
    got_ub = W("vector", lambda v, b, src=big[lot % 3]: v.tensor_copy(u_bias[:, :], src[:, :]), [t])
    big_free[lot % 3] = got_ub
    lot += 1

    for b0 in range(NB):
        half, buf = b0 // (NB // 2), stage_buf[b0 // (NB // 2)]

        def value_side(pe, b, b0=b0, dst=big[lot % 3]):
            for k in range(2):
                for par in range(2):
                    last = pe.matmul(dst[par * T2:(par + 1) * T2, k * 512:(k + 1) * 512],
                                     ctx[:, b0 * T2:(b0 + 1) * T2],
                                     hh[:, par, 4 * k:4 * k + 4, :].rearrange("p q d -> p (q d)"),
                                     start=True, stop=True)
            return last
        t = W("tensor", value_side, [*got_h, got_ctx, big_free[lot % 3]])
        t = W("vector", lambda v, b, b0=b0, buf=buf, src=big[lot % 3]: v.tensor_tensor(
            buf[:, b0 % (NB // 2), :], src[:, :], u_bias[:, :], ALU.add), [t, stored[half], got_ub])
        big_free[lot % 3] = t
        lot += 1
        if b0 % (NB // 2) == NB // 2 - 1:
            plan.dma("sync", "W", "u_out", lambda e, b, half=half, buf=buf: e.dma_start(
                g["u_all"][half * NB // 2:(half + 1) * NB // 2].rearrange("b p n -> p b n"), buf[:, :, :]), [t])

    def part(hi, lo, raw, after):
        t = W("gpsimd", lambda e, b: e.tensor_copy(hi, raw), after)
        return W("vector", lambda v, b: v.tensor_tensor(lo, raw, f32(hi), ALU.subtract), [t])
    part(g["wqk_hi"][:, :, :], g["wqk_lo"][:, :, :], wqk_raw[:, :, :], [got_wqk])
    for e0 in range(NE):
        if e0 == NE // 2:
            got_w1 = plan.dma("sync", "W", "w1_b", lambda e, b: e.dma_start(
                w1_raw[:, :, :], g["w1"][:, NE // 2:, :]), [t])
        t = part(w1_hi[:, e0, :], w1_lo[:, e0, :], w1_raw[:, e0 % (NE // 2), :], [got_w1])
    plan.finish()

    sems = {n: nc.alloc_semaphore(n + "_w") for n in plan.counts}
    with nc.Block() as block:
        for name in ("sync", "gpsimd", "vector", "scalar", "tensor"):
            def body(eng, name=name):
                plan.emit(eng, queues.get(name, []), sems, 0, False)
                if name == "sync":
                    for s in ("dma_r_out", "dma_a_out0", "dma_a_out1", "dma_u_out", "dma_rest"):
                        eng.wait_ge(sems[s], plan.per_batch[s])
            getattr_free = {"sync": block.sync, "gpsimd": block.gpsimd, "vector": block.vector,
                            "scalar": block.scalar, "tensor": block.tensor}
            getattr_free[name](body)


def main(nc, stack, sb, big, small, g):
    ident, minus_half = g["ident"], g["minus_half"]

    x_in = sb("x_in", [P, ST, D])
    x_keep = sb("x_keep", [P, ST, D])
    xn = sb("xn", [P, ST, D])
    stats_a, moments_a, rstd_a = sb("stats_a", [P, ST, 6]), sb("moments_a", [P, ST, 2]), sb("rstd_a", [P, ST])
    xt, xt_hi, xt_lo = sb("xt", [P, S]), sb("xt_hi", [P, S], F32R), sb("xt_lo", [P, S], F32R)
    parts = sb("parts", [P, NPIECE, 2, S], BF16)
    rest = sb("rest", [P, 2 * S])
    v_cols = sb("v_cols", [P, ST, NH, 32])
    q_stack = sb("q_stack", [P, NH, S], BF16)
    k_stack = sb("k_stack", [P, NH, S], BF16)
    max_a = sb("max_a", [P, ST, NH])
    max_parts = sb("max_parts", [NH, NPIECE, S], BF16)
    max_rest = sb("max_rest", [NH, S])
    NPROB = 3
    probs = [sb(f"probs{n}", [P, 4, S]) for n in range(NPROB)]
    o_cols = sb("o_cols", [P, 4, S])
    rec_a = sb("rec_a", [P, ST, NH])
    attn = sb("attn", [P, ST, NH, DK])
    attn_t = sb("attn_t", [P, S])
    x2, x2_bo, xn2, x2t = sb("x2", [P, ST, D]), sb("x2_bo", [P, ST, D]), sb("xn2", [P, ST, D]), sb("x2t", [P, S])
    stats_b, moments_b, rstd_b = sb("stats_b", [P, ST, 6]), sb("moments_b", [P, ST, 2]), sb("rstd_b", [P, ST])
    a_b, u_b = sb("a_b", [P, NX * T2]), sb("u_b", [P, NPAIR, D])
    r_b = sb("r_b", [NPIECE, NX * T2], BF16)
    mask_i = sb("mask_i", [P, ST, T2], I32)
    mask_neg = sb("mask_neg", [P, ST, T2])
    any_b = sb("any_b", [P, ST])
    s_b = sb("s_b", [P, ST, NX, T2])
    max_b, rec_b = sb("max_b", [P, ST, NX]), sb("rec_b", [P, ST, NX])
    p_t = sb("p_t", [P, NPAIR, S])
    x3, xn3, x3t = sb("x3", [P, ST, D]), sb("xn3", [P, ST, D]), sb("x3t", [P, S])
    x3_hi, x3_lo = sb("x3_hi", [P, S], F32R), sb("x3_lo", [P, S], F32R)
    logits, top_v = sb("logits", [P, ST, NE]), sb("top_v", [P, ST, NE])
    top_i, top_if = sb("top_i", [P, ST, NE], U32), sb("top_if", [P, ST, 2])
    gate = sb("gate", [P, 4, ST])
    cw2 = sb("cw2", [P, 2, ST, NE])
    cw = sb("cw", [P, ST, NE])
    cw_t = sb("cw_t", [NE, S])
    acc = sb("acc", [P, ST, D])
    hidden = [sb(f"hidden{n}", [P, FB, S]) for n in range(2)]

    plan = Plan()

    def iteration(has):
        plan.start()
        on_small = [0, [None, None]]
        if "B" in has or "C" in has:
            on_small[1] = [Done("vector_B", 0, END)] * 2

        def take_small():
            n = on_small[0] % 2
            on_small[0] += 1
            return n, small[n], on_small[1][n]

        def free_small(n, done):
            on_small[1][n] = done

        last_of = {}
        big2 = {"free": None}

        def stage_a():
            A = lambda engine, make, after=(): plan.step(engine, "A", make, after)
            before = lambda d: Done(d.sem, d.lead - 1, d.count)
            prev = lambda engine: Done(f"{engine}_A", 1, END)
            got_x = plan.dma("sync", "A", "x", lambda e, b: e.dma_start(
                x_in[:, :, :], g["x"][b].rearrange("(n p) d -> p n d", p=P)),
                [plan.before("x normalised"), plan.before("x kept")])
            t_n = layer_norm(plan, "A", x_in, xn, stats_a, moments_a, rstd_a, minus_half, [got_x], [])
            plan.name("x normalised", t_n)
            yield "norm"
            n, ps_t, free = take_small()
            t = transpose_tiles(plan, "A", ps_t, xn, ident, [t_n, free])
            t_xt = A("scalar", lambda a, b: a.activation(xt[:, :], ps_t[:, 0:S], ACT.Copy), [t])
            t_hi = A("vector", lambda v, b: v.tensor_copy(xt_hi[:, :], xt[:, :]), [t_xt])
            t_lo = A("vector", lambda v, b: v.tensor_tensor(xt_lo[:, :], xt[:, :], f32(xt_hi[:, :]),
                                                           ALU.subtract), [t_hi])
            free_small(n, t_xt)
            yield "turn"
            n, ps_qk, free = take_small()

            def project(pe, b):
                for c in range(2):
                    last = three_passes(pe, ps_qk[:, c * S:(c + 1) * S], g["wqk_hi"][:, c, :], g["wqk_lo"][:, c, :],
                                        xt_hi[:, :], xt_lo[:, :])
                return last
            t_qk = A("tensor", project, [t_lo, free])
            t = A("vector", lambda v, b: v.tensor_copy(
                parts[:, 0, :, :].rearrange("p c s -> p (c s)"), ps_qk[:, :]), [t_qk])
            t = A("vector", lambda v, b: v.tensor_tensor(
                rest[:, :], ps_qk[:, :], parts[:, 0, :, :].rearrange("p c s -> p (c s)"), ALU.subtract), [t])
            free_small(n, t)
            t = A("vector", lambda v, b: v.tensor_copy(
                parts[:, 1, :, :].rearrange("p c s -> p (c s)"), rest[:, :]), [t])
            t = A("vector", lambda v, b: v.tensor_tensor(
                parts[:, 2, :, :].rearrange("p c s -> p (c s)"), rest[:, :],
                parts[:, 1, :, :].rearrange("p c s -> p (c s)"), ALU.subtract), [t])
            for c in range(2):
                t_w = plan.dma("sync", "A", "parts_out", lambda e, b, c=c: e.dma_start(
                    g["parts_dram"][c].rearrange("k p s -> p k s"), parts[:, :, c, :]), [t])
            for a in range(NPIECE):
                t_st = plan.dma("sync", "A", "stacks", lambda e, b, a=a: e.dma_start(
                    q_stack[a * 24:(a + 1) * 24, :, :],
                    g["parts_dram"][0].rearrange("k (d h) s -> (k d) h s", d=DK)), [t_w, prev("tensor")])
                for k in range(NPIECE):
                    t_st = plan.dma("sync", "A", "stacks", lambda e, b, a=a, k=k: e.dma_start(
                        k_stack[a * 24 + k * 8:a * 24 + k * 8 + 8, :, :],
                        g["parts_dram"][1, a].rearrange("(d h) s -> d h s", d=DK)), [t_w, prev("tensor")])
            n, ps_v, free = take_small()

            def values(pe, b):
                for m in range(ST):
                    last = pe.matmul(ps_v[:, m * P:(m + 1) * P], xt[:, m * P:(m + 1) * P], g["wv_wo"][:, 0, :],
                                     start=True, stop=True)
                return last
            t = A("tensor", values, [t_xt, free])
            t_v = A("scalar", lambda a, b: a.activation(
                v_cols[:, :, :, 0:DK], ps_v[:, 0:ST * P].rearrange("p (m h d) -> p m h d", m=ST, h=NH),
                ACT.Copy), [t, prev("tensor")])
            free_small(n, t_v)
            yield "qkv"
            for m in range(ST):
                for h0 in range(0, NH, 4):
                    def scores(pe, b, m=m, h0=h0):
                        for h in range(h0, h0 + 4):
                            last = pe.matmul(big[2][:, (h - h0) * S:(h - h0 + 1) * S],
                                             q_stack[0:ROWS, h, m * P:(m + 1) * P], k_stack[0:ROWS, h, :],
                                             start=True, stop=True)
                        return last
                    t = A("tensor", scores, [t_st, big2["free"]])
                    t_mx = big2["free"] = A("vector", lambda v, b, m=m, h0=h0: v.tensor_reduce(
                        max_a[:, m, h0:h0 + 4], big[2][:, :].rearrange("p (h t) -> p h t", h=4),
                        AX.X, ALU.max), [t])
                    if (m, h0) == (0, 0):
                        plan.name("x kept", A("scalar", lambda a, b: a.activation(
                            x_keep[:, :, :], x_in[:, :, :], ACT.Copy), [got_x, last_of.get("x2")]))
                    yield f"max{m * 4 + h0 // 4}"
            n, ps_m, free = take_small()

            def turn_max(pe, b):
                for m in range(ST):
                    last = pe.transpose(ps_m[0:NH, m * P:(m + 1) * P], max_a[:, m, :], ident[:, :])
                return last
            t = A("tensor", turn_max, [t_mx, free])
            t = A("vector", lambda v, b: v.tensor_scalar(
                max_parts[:, 0, :], ps_m[0:NH, 0:S], -1.0, None, ALU.mult), [t])
            t = A("vector", lambda v, b: v.scalar_tensor_tensor(
                max_rest[:, :], ps_m[0:NH, 0:S], -1.0, max_parts[:, 0, :], ALU.mult, ALU.subtract), [t])
            free_small(n, t)
            t = A("vector", lambda v, b: v.tensor_copy(max_parts[:, 1, :], max_rest[:, :]), [t])
            t = A("vector", lambda v, b: v.tensor_tensor(
                max_parts[:, 2, :], max_rest[:, :], max_parts[:, 1, :], ALU.subtract), [t])
            for k in range(NPIECE):
                t_m = plan.dma("sync", "A", "max_rows", lambda e, b, k=k: e.dma_start(
                    q_stack[ROWS + k:ROWS + k + 1, :, :], max_parts[:, k, :]), [t])
            yield "turn max"
            t_exp, t_s = [None] * 8, [None] * 8
            t_pv = [None] * 8
            big_free = [None, None]

            def by_key(u):
                h0, m = 4 * (u // ST), u % ST
                ps = big[u % 2]

                def make(pe, b):
                    for h in range(h0, h0 + 4):
                        last = pe.matmul(ps[:, (h - h0) * S:(h - h0 + 1) * S],
                                         k_stack[0:ROWS + NPIECE, h, m * P:(m + 1) * P],
                                         q_stack[0:ROWS + NPIECE, h, :], start=True, stop=True)
                    return last
                t_s[u] = A("tensor", make, [t_m, big_free[u % 2]])
                t_exp[u] = A("scalar", lambda a, b: a.activation(
                    probs[u % NPROB][:, :, :].rearrange("p h s -> p (h s)"), ps[:, :], ACT.Exp, scale=SCALE_A),
                    [t_s[u], t_pv[u - NPROB] if u >= NPROB else None])
                big_free[u % 2] = t_exp[u]

            def times_v(u):
                h0, m = 4 * (u // ST), u % ST

                def make(pe, b):
                    for h in range(h0, h0 + 4):
                        j = h - h0
                        last = pe.matmul(big[2][32 * j:32 * j + 32, (h0 // 4) * S:(h0 // 4 + 1) * S],
                                         v_cols[:, m, h, :], probs[u % NPROB][:, j, :],
                                         start=(m == 0), stop=(m == ST - 1))
                    return last
                t_pv[u] = A("tensor", make, [t_exp[u], t_v])

            by_key(0)
            by_key(1)
            for u in range(8):
                times_v(u)
                if u + 2 < 8:
                    by_key(u + 2)
                yield f"values{u}"

        def stage_b():
            B = lambda engine, make, after=(): plan.step(engine, "B", make, after)
            prev = lambda engine: Done(f"{engine}_B", 0, END)
            got_a = plan.dma("sync", "B", "a_in", lambda e, b: e.dma_start(a_b[:, :], g["a_all"][b]),
                             [plan.before("scores")])
            got_r = plan.dma("sync", "B", "r_in", lambda e, b: e.dma_start(
                r_b[:, :].rearrange("k (h t) -> k h t", t=T2), g["r_all"][:, b]), [plan.before("scores")])
            got_mask = plan.dma("sync", "B", "mask_in", lambda e, b: e.dma_start(
                mask_i[:, :, :], g["mask"][b].rearrange("(n p) t -> p n t", p=P)), [plan.before("mask")])
            got_u = plan.dma("sync", "B", "u_in", lambda e, b: e.dma_start(
                u_b[:, :, :], g["u_all"][b].rearrange("p (q d) -> p q d", d=D)), [plan.before("times u")])
            t = B("scalar", lambda a, b: a.activation(
                o_cols[:, :, :].rearrange("p q s -> p (q s)"), big[2][:, :], ACT.Copy), [Done("tensor_A", 1, END)])
            big2["free"] = t
            yield "sums"
            for m in range(ST):
                n, ps, free = take_small()

                def turn(pe, b, ps=ps, m=m):
                    for q in range(4):
                        last = pe.transpose(ps[:, q * P:(q + 1) * P], o_cols[:, q, m * P:(m + 1) * P], ident[:, :])
                    return last
                t1 = B("tensor", turn, [t, free])
                cols = ps[:, :].rearrange("p (h w) -> p h w", w=32)
                t2 = B("vector", lambda v, b, m=m, cols=cols: v.reciprocal(rec_a[:, m, :], cols[:, :, DK]), [t1])
                t_at = B("vector", lambda v, b, m=m, cols=cols: v.tensor_tensor(
                    attn[:, m, :, :], cols[:, :, 0:DK], rec_a[:, m, :].unsqueeze(2).to_broadcast([P, NH, DK]),
                    ALU.mult), [t2])
                free_small(n, t_at)
            yield "normalise"
            n, ps1, free = take_small()
            t = transpose_tiles(plan, "B", ps1, attn[:, :, :, :].rearrange("p m h d -> p m (h d)"), ident,
                                [t_at, free])
            t = B("scalar", lambda a, b: a.activation(attn_t[:, :], ps1[:, 0:S], ACT.Copy), [t])
            free_small(n, t)
            yield "turn"
            n, ps2, free = take_small()

            def project(pe, b):
                for m in range(ST):
                    last = pe.matmul(ps2[:, m * P:(m + 1) * P], attn_t[:, m * P:(m + 1) * P], g["wv_wo"][:, 1, :],
                                     start=True, stop=True)
                return last
            t = B("tensor", project, [t, free])
            t = last_of["x2"] = B("vector", lambda v, b: v.tensor_tensor(
                x2[:, :, :], ps2[:, 0:S].rearrange("p (m d) -> p m d", m=ST), x_keep[:, :, :], ALU.add),
                [t, plan.before("x kept")])
            free_small(n, t)
            t_bo = B("gpsimd", lambda e, b: e.tensor_tensor(
                x2_bo[:, :, :], x2[:, :, :], g["bo_all"][:, :].unsqueeze(1).to_broadcast([P, ST, D]), ALU.add), [t])
            t_n = layer_norm(plan, "B", x2, xn2, stats_b, moments_b, rstd_b, minus_half, [t], [])
            t_mk = B("vector", lambda v, b: v.tensor_scalar(
                mask_neg[:, :, :], mask_i[:, :, :], 0.0, MASKED / SCALE_B, ALU.is_equal, ALU.mult), [got_mask])
            plan.name("mask", t_mk)
            t = B("vector", lambda v, b: v.tensor_reduce(any_b[:, :], mask_neg[:, :, :], AX.X, ALU.max), [t_mk])
            t_any = B("vector", lambda v, b: v.tensor_scalar(
                any_b[:, :], any_b[:, :], 0.0, None, ALU.is_equal), [t])
            yield "project"
            n, ps3, free = take_small()
            t = transpose_tiles(plan, "B", ps3, xn2, ident, [t_n, free])
            t_xt = B("scalar", lambda a, b: a.activation(x2t[:, :], ps3[:, 0:S], ACT.Copy), [t])
            free_small(n, t_xt)
            yield "turn x2"
            t_sub = [None] * ST
            for m in range(ST):
                def scores(pe, b, m=m):
                    for k in range(2):
                        cols = slice(k * 512, (k + 1) * 512)
                        pe.matmul(big[2][:, cols], x2t[:, m * P:(m + 1) * P], a_b[:, cols], start=True, stop=False)
                        last = pe.matmul(big[2][:, cols], g["ones_row"][:, :], r_b[:, cols],
                                         start=False, stop=True)
                    return last
                t = B("tensor", scores, [t_xt, got_a, got_r, big2["free"]])
                plan.name("scores", t)
                t = big2["free"] = B("vector", lambda v, b, m=m: v.tensor_tensor(
                    s_b[:, m, :, :], big[2][:, :].rearrange("p (h t) -> p h t", h=NX),
                    mask_neg[:, m, :].unsqueeze(1).to_broadcast([P, NX, T2]), ALU.add), [t, t_mk])
                t = B("vector", lambda v, b, m=m: v.tensor_reduce(
                    max_b[:, m, :], s_b[:, m, :, :], AX.X, ALU.max), [t])
                t_sub[m] = B("gpsimd", lambda e, b, m=m: e.tensor_tensor(
                    s_b[:, m, :, :], s_b[:, m, :, :], max_b[:, m, :].unsqueeze(2).to_broadcast([P, NX, T2]),
                    ALU.subtract), [t])
                yield f"scores{m}"
            t_p = [None] * ST
            for m in range(ST):
                t = B("scalar", lambda a, b, m=m: a.activation(
                    s_b[:, m, :, :], s_b[:, m, :, :], ACT.Exp, scale=SCALE_B), [t_sub[m]])
                t = B("vector", lambda v, b, m=m: v.tensor_reduce(
                    rec_b[:, m, :], s_b[:, m, :, :], AX.X, ALU.add), [t])
                t = B("vector", lambda v, b, m=m: v.reciprocal(rec_b[:, m, :], rec_b[:, m, :]), [t])
                t = B("vector", lambda v, b, m=m: v.tensor_scalar(
                    rec_b[:, m, :], rec_b[:, m, :], any_b[:, m:m + 1], None, ALU.mult), [t, t_any])
                t_p[m] = B("vector", lambda v, b, m=m: v.tensor_tensor(
                    s_b[:, m, :, :], s_b[:, m, :, :], rec_b[:, m, :].unsqueeze(2).to_broadcast([P, NX, T2]),
                    ALU.mult), [t])
            yield "exp"
            t_pt = []
            for m in range(ST):
                for q0 in range(0, NPAIR, 4):
                    n, ps, free = take_small()

                    def turn(pe, b, ps=ps, m=m, q0=q0):
                        for q in range(4):
                            last = pe.transpose(
                                ps[:, q * P:(q + 1) * P],
                                s_b[:, m, 2 * (q0 + q):2 * (q0 + q) + 2, :].rearrange("p h t -> p (h t)"), ident[:, :])
                        return last
                    t = B("tensor", turn, [t_p[m], free])
                    to = p_t[:, q0:q0 + 4, m * P:(m + 1) * P]
                    src = ps[:, :].rearrange("p (q s) -> p q s", q=4)
                    t = B("vector", lambda v, b, to=to, src=src: v.tensor_copy(to, src), [t])
                    free_small(n, t)
                    t_pt.append(t)
                yield f"turn p{m}"
            n, ps4, free = take_small()

            def times_u(pe, b):
                for m in range(ST):
                    for q in range(NPAIR):
                        last = pe.matmul(ps4[:, m * P:(m + 1) * P], p_t[:, q, m * P:(m + 1) * P], u_b[:, q, :],
                                         start=(q == 0), stop=(q == NPAIR - 1))
                return last
            t = B("tensor", times_u, [*t_pt, got_u, free])
            plan.name("times u", t)
            t_x3 = B("vector", lambda v, b: v.tensor_tensor(
                x3[:, :, :], ps4[:, 0:S].rearrange("p (m d) -> p m d", m=ST), x2_bo[:, :, :], ALU.add),
                [t, t_bo, last_of.get("x3 read")])
            plan.name("x3", t_x3)
            free_small(n, t_x3)
            t_n = layer_norm(plan, "B", x3, xn3, stats_b, moments_b, rstd_b, minus_half, [t_x3], [])
            yield "times u"
            n, ps5, free = take_small()
            t = transpose_tiles(plan, "B", ps5, xn3, ident, [t_n, free])
            t_xt = plan.name("x3t", B("scalar", lambda a, b: a.activation(x3t[:, :], ps5[:, 0:S], ACT.Copy),
                                      [t, last_of.get("routed")]))
            free_small(n, t_xt)
            t = B("vector", lambda v, b: v.tensor_copy(x3_hi[:, :], x3t[:, :]), [t_xt, last_of.get("up")])
            plan.name("x3 parts", B("vector", lambda v, b: v.tensor_tensor(
                x3_lo[:, :], x3t[:, :], f32(x3_hi[:, :]), ALU.subtract), [t]))
            yield "turn x3"

        def stage_c():
            C = lambda engine, make, after=(): plan.step(engine, "C", make, after)
            parts_3, got_x3t, got_x3 = plan.before("x3 parts"), plan.before("x3t"), plan.before("x3")
            t_up, t_gelu, t_down = {}, {}, {}

            def up(e0):
                ps = big[e0 % 2]

                def make(pe, b):
                    for f in range(FB):
                        cols = slice(f * P, (f + 1) * P)
                        last = three_passes(pe, ps[:, f * S:(f + 1) * S], g["w1_hi"][:, e0, cols],
                                            g["w1_lo"][:, e0, cols], x3_hi[:, :], x3_lo[:, :])
                    return last
                t_up[e0] = last_of["up"] = C("tensor", make, [parts_3, t_gelu.get(e0 - 2)])

                def gelu(a, b):
                    for f in range(FB):
                        last = a.activation(hidden[e0 % 2][:, f, :], ps[:, f * S:(f + 1) * S], ACT.Gelu,
                                            bias=g["b1_sb"][:, e0 * FB + f:e0 * FB + f + 1])
                    return last
                t_gelu[e0] = C("scalar", gelu, [t_up[e0], t_down.get(e0 - 2)])

            up(0)
            yield "up0"
            n, ps6, free = take_small()

            def route(pe, b):
                for m in range(ST):
                    last = pe.matmul(ps6[:, m * NE:(m + 1) * NE], x3t[:, m * P:(m + 1) * P], g["wr"][:, :],
                                     start=True, stop=True)
                return last
            t = last_of["routed"] = C("tensor", route, [got_x3t, free])
            t = C("vector", lambda v, b: v.tensor_copy(
                logits[:, :, :].rearrange("p m e -> p (m e)"), ps6[:, 0:ST * NE]), [t])
            free_small(n, t)

            def largest(v, b):
                for m in range(ST):
                    last = v.max(top_v[:, m, :], logits[:, m, :])
                return last

            def places(v, b):
                for m in range(ST):
                    last = v.max_index(top_i[:, m, :], top_v[:, m, :], logits[:, m, :])
                return last
            t = plan.step("vector", "C", largest, [t], apart=True)
            t_i = plan.step("vector", "C", places, [t], apart=True)
            t = C("vector", lambda v, b: v.tensor_tensor(
                gate[:, 0, :], top_v[:, :, 1], top_v[:, :, 0], ALU.subtract), [t])
            t_e = C("gpsimd", lambda e, b: e.tensor_tensor(
                gate[:, 1, :], g["euler"][:, :], gate[:, 0, :], ALU.pow), [t])
            t_if = C("vector", lambda v, b: v.tensor_copy(top_if[:, :, :], top_i[:, :, 0:2]), [t_i])
            t = C("vector", lambda v, b: v.tensor_scalar(gate[:, 2, :], gate[:, 1, :], 1.0, None, ALU.add), [t_e])
            t = C("vector", lambda v, b: v.reciprocal(gate[:, 2, :], gate[:, 2, :]), [t])
            t = C("vector", lambda v, b: v.tensor_tensor(
                gate[:, 3, :], gate[:, 1, :], gate[:, 2, :], ALU.mult), [t])

            def weigh(v, b):
                for k in range(2):
                    for m in range(ST):
                        last = v.tensor_scalar(cw2[:, k, m, :], g["iota8"][:, :], top_if[:, m, k:k + 1],
                                               gate[:, 2 + k, m:m + 1], ALU.is_equal, ALU.mult)
                return last
            t = C("vector", weigh, [t, t_if])
            t_cw = C("vector", lambda v, b: v.tensor_tensor(
                cw[:, :, :], cw2[:, 0, :, :], cw2[:, 1, :, :], ALU.add), [t])
            yield "route"

            t_mix = [t_cw] * ST

            def down(e0):
                n, ps, free = take_small()

                def make(pe, b):
                    for m in range(ST):
                        for f in range(FB):
                            last = pe.matmul(ps[:, m * P:(m + 1) * P], hidden[e0 % 2][:, f, m * P:(m + 1) * P],
                                             g["w2_sb"][:, e0, f, :], start=(f == 0), stop=(f == FB - 1))
                    return last
                t_down[e0] = C("tensor", make, [t_gelu[e0], free])
                so_far = x3 if e0 == 0 else acc
                for m in range(ST):
                    t_mix[m] = C("vector", lambda v, b, m=m: v.scalar_tensor_tensor(
                        acc[:, m, :], ps[:, m * P:(m + 1) * P], cw[:, m, e0:e0 + 1], so_far[:, m, :],
                        ALU.mult, ALU.add), [t_down[e0], t_mix[m], got_x3, plan.before("stored") if e0 == 0 else None])
                if e0 == 0:
                    last_of["x3 read"] = t_mix[ST - 1]
                free_small(n, t_mix[ST - 1])

            for e0 in range(NE):
                if e0 + 1 < NE:
                    up(e0 + 1)
                    yield f"up{e0 + 1}"
                down(e0)
                if e0 == 3:
                    n, ps7, free = take_small()

                    def turn_cw(pe, b):
                        for m in range(ST):
                            last = pe.transpose(ps7[0:NE, m * P:(m + 1) * P], cw[:, m, :], ident[:, :])
                        return last
                    t = C("tensor", turn_cw, [t_cw, free])
                    t_cwt = C("vector", lambda v, b: v.tensor_copy(cw_t[:, :], ps7[0:NE, 0:S]), [t])
                    free_small(n, t_cwt)
                if e0 == 4:
                    n, ps8, free = take_small()

                    def bias2(pe, b):
                        for m in range(ST):
                            last = pe.matmul(ps8[:, m * P:(m + 1) * P], cw_t[:, m * P:(m + 1) * P],
                                             g["b2_sb"][:, :], start=True, stop=True)
                        return last
                    t = C("tensor", bias2, [t_cwt, free])
                    t_mix = [C("vector", lambda v, b: v.tensor_tensor(
                        acc[:, :, :], ps8[:, 0:S].rearrange("p (m d) -> p m d", m=ST), acc[:, :, :], ALU.add),
                        [t, *t_mix])] * ST
                    free_small(n, t_mix[0])
                yield f"down{e0}"
            plan.name("stored", plan.dma("gpsimd", "C", "out", lambda e, b: e.dma_start(
                g["out"][b].rearrange("(n p) d -> p n d", p=P), acc[:, :, :]), t_mix))

        order = ORDER
        running = {"A": stage_a(), "B": stage_b(), "C": stage_c()}
        for stage, until in order:
            if stage in has:
                for label in running[stage]:
                    if label == until:
                        break
        for stage in has:
            assert next(running[stage], None) is None, stage
        queues = plan.queues
        plan.finish()
        return queues

    iteration("ABC")
    segments = [(-2, iteration("A")), (-1, iteration("AB")), ("loop", iteration("ABC")),
                (NB - 2, iteration("BC")), (NB - 1, iteration("C"))]

    sems = {n: nc.alloc_semaphore(n) for n in plan.per_batch}
    ready = nc.alloc_semaphore("constants")

    with nc.Block() as block:
        def run(name):
            def body(eng):
                if name == "vector":
                    eng.memset(k_stack[64:96, :, :], 1.0).then_inc(ready, 1)
                    eng.memset(v_cols[:, :, :, :], 0.0).then_inc(ready, 1)
                    eng.wait_ge(ready, 2)
                    eng.memset(v_cols[:, :, :, DK:DK + 1], 1.0).then_inc(ready, 1)
                eng.wait_ge(ready, 3)
                for j, queues in segments:
                    queue = queues.get(name, [])
                    if not queue:
                        continue
                    if j == "loop":
                        with eng.Fori(0, NB - 2) as reg:
                            plan.emit(eng, queue, sems, reg, True, g["spare"][:, :])
                    else:
                        plan.emit(eng, queue, sems, j, False)
                if name == "gpsimd":
                    eng.wait_ge(sems["dma_out"], NB * plan.per_batch["dma_out"])
            return body
        block.sync(run("sync"))
        block.gpsimd(run("gpsimd"))
        block.vector(run("vector"))
        block.scalar(run("scalar"))
        block.tensor(run("tensor"))


def kernel(x, ctx_1024, mask_BxSxS2_ik1, L0_attn_W_q, L0_attn_W_k, L0_attn_W_v, L0_attn_W_out, L0_xattn_Wq,
           L0_xattn_bq, L0_xattn_Wk, L0_xattn_bk, L0_xattn_Wv, L0_xattn_bv, L0_xattn_Wo, L0_xattn_bo,
           L0_ffn_w_router, L0_ffn_w1, L0_ffn_b1, L0_ffn_w2, L0_ffn_b2):
    import concourse.bacc as bacc
    from concourse.bass_utils import run_bass_kernel_spmd

    A = np.asarray
    by_head = lambda w: A(w).reshape(NX, DX, D).transpose(1, 0, 2)
    turned = lambda w: A(w).reshape(NH, DK, D).transpose(2, 1, 0).reshape(D, P)
    arrays = {
        "x": A(x),
        "ctx_t": A(ctx_1024).reshape(NB * T2, D).T,
        "mask": A(mask_BxSxS2_ik1),
        "attn_w": np.stack([turned(L0_attn_W_q), turned(L0_attn_W_k), A(L0_attn_W_v).T, A(L0_attn_W_out).T], 1),
        "xq": by_head(L0_xattn_Wq),
        "xk": by_head(L0_xattn_Wk),
        "xv": by_head(L0_xattn_Wv),
        "xo": A(L0_xattn_Wo).reshape(D, NX, DX).transpose(2, 1, 0),
        "xbias": np.stack([A(v).reshape(NX, DX).T for v in (L0_xattn_bq, L0_xattn_bk, L0_xattn_bv)], 1),
        "bo": A(L0_xattn_bo),
        "w_router": A(L0_ffn_w_router).T,
        "w1": A(L0_ffn_w1).transpose(2, 0, 1),
        "b1": A(L0_ffn_b1).reshape(NE * FB, P).T,
        "w2": A(L0_ffn_w2).reshape(NE, D, FB, P).transpose(3, 0, 2, 1),
        "b2": A(L0_ffn_b2),
    }
    arrays = {n: np.ascontiguousarray(a) for n, a in arrays.items()}
    nc = bacc.Bacc("TRN2", target_bir_lowering=False, num_devices=1)
    aps = {n: nc.dram_tensor(n, a.shape, mybir.dt.from_np(a.dtype), kind="ExternalInput").ap()
           for n, a in arrays.items()}
    out = nc.dram_tensor("out", (NB, S, D), F32, kind="ExternalOutput").ap()
    build(nc, *aps.values(), out)
    r = run_bass_kernel_spmd(nc, [arrays], core_ids=[0])
    return r.results[0]["out"]
```

```python
from contextlib import ExitStack

import concourse.bass as bass
import concourse.mybir as mybir
import numpy as np

F32, F32R, BF16 = mybir.dt.float32, mybir.dt.float32r, mybir.dt.bfloat16
I32, U32 = mybir.dt.int32, mybir.dt.uint32
ALU, ACT, AX = mybir.AluOpType, mybir.ActivationFunctionType, mybir.AxisListType

P = 128
NB, S, D = 16, 256, 128
ST = S // P
NH, DK = 16, 8
T2, DX = 64, 64
NX = 16
NPAIR = NX // 2
NE, FF = 8, 512
FB = FF // P
NPIECE = 3
ROWS = NPIECE * NPIECE * DK
EPS = 1e-5
MASKED = -1e20
SCALE_A, SCALE_B = DK ** -0.5, DX ** -0.5
END = "end"
NBUF = 2
SUMS = 2

ORDER = [[x.split(":") for x in part.split()] for part in (
    "L:load W:load0 W:load1 W:const W:wqk L:norm W:ctx W:fold0 W:fold1 L:turn W:vectors W:rows L:qk "
    "L:parts L:end W:fold_v0 W:fold_v1 | "
    "A:stacks A:v W:bias A:max0 W:key00 A:max1 W:key01 W:key02 W:key03 A:max2 A:max3 W:value0 W:value1 "
    "W:value2 W:value3 W:store0 A:max4 W:key10 L:load W:key11 W:key12 A:max5 W:key13 A:max6 W:value4 "
    "A:max7 W:value5 W:value6 A:turn_max W:value7 W:store1 W:key20 W:key21 W:key22 W:key23 A:key0 "
    "W:value8 W:value9 A:key1 W:value10 A:values0 A:key2 A:values1 A:key3 L:norm A:values2 A:key4 "
    "A:values3 A:key5 L:turn A:values4 A:key6 W:value11 L:qk W:store2 A:values5 A:key7 W:key30 L:parts "
    "W:key31 A:values6 W:key32 W:key33 L:end W:value12 A:values7 A:end | "
    "A:stacks W:value13 W:value14 L:load W:value15 A:v L:norm W:store3 A:max0 W:experts L:turn A:max1 "
    "A:max2 A:max3 L:qk W:w1_0 B:load W:w1_1 B:sums B:normalise A:max4 W:w1_2 W:w1_3 M:load M:shift "
    "A:max5 B:turn A:max6 W:w1_b M:a A:max7 A:turn_max B:project B:turn_x2 W:w1_4 B:scores0 B:scores1 "
    "A:key0 L:parts L:end A:key1 B:exp0 A:values0 B:exp1 A:key2 A:values1 B:turn_p00 A:key3 B:turn_p01 "
    "A:values2 A:key4 A:values3 A:key5 B:turn_p10 B:turn_p11 W:w1_5 A:values4 W:w1_6 B:times_u A:key6 "
    "W:w1_7 B:norm3 W:end A:values5 A:key7 B:turn_x3 A:values6 B:end A:values7 A:end | "
    "L:load A:stacks B:load L:norm B:sums M:load A:v C:up0 B:normalise C:route C:up1 B:turn A:max0 "
    "M:shift C:down0 C:up2 A:max1 C:down1 A:max2 A:max3 B:project M:a C:up3 C:down2 A:max4 C:up4 C:down3 "
    "A:max5 C:turn_cw A:max6 L:turn C:up5 B:turn_x2 A:max7 C:down4 C:bias2 C:up6 A:turn_max B:scores0 "
    "C:down5 C:up7 B:scores1 C:down6 B:exp0 A:key0 A:key1 C:down7 A:values0 B:exp1 A:key2 A:values1 "
    "B:turn_p00 A:key3 A:values2 A:key4 A:values3 A:key5 B:turn_p01 B:turn_p10 B:turn_p11 L:qk B:times_u "
    "A:values4 L:parts A:key6 C:end A:values5 A:key7 L:end B:norm3 A:values6 B:turn_x3 A:values7 A:end "
    "B:end | "
    "C:up0 M:load C:route C:up1 B:load M:shift C:down0 B:sums C:up2 M:a B:normalise B:turn C:down1 "
    "B:project C:up3 C:down2 B:turn_x2 C:up4 B:scores0 C:down3 B:scores1 C:turn_cw C:up5 C:down4 C:bias2 "
    "B:exp0 B:exp1 C:up6 C:down5 C:up7 C:down6 B:turn_p00 B:turn_p01 B:turn_p10 B:turn_p11 C:down7 C:end "
    "B:times_u B:norm3 B:turn_x3 B:end").split("|")]


class Done:

    def __init__(self, sem, lead, count):
        self.sem, self.lead, self.count = sem, lead, count


class Plan:

    LEAD = {"L": 3, "A": 2, "M": 1, "B": 1, "C": 0, "W": None}

    def __init__(self):
        self.per_batch, self.points, self.once_counts = {}, {}, {}
        self.start()

    def start(self):
        self.counts, self.queues = {}, {}
        return self.queues

    def name(self, point, done):
        self.points[point] = done
        return done

    def before(self, point):
        d = self.points.get(point)
        return d and Done(d.sem, d.lead - 1, d.count)

    def once(self, point):
        return self.points[point]

    def finish(self):
        for sem, n in self.counts.items():
            assert self.per_batch.setdefault(sem, n) == n, sem

    def step(self, engine, stage, make, after=(), sem=None, add=1, apart=False):
        sem = sem or f"{engine}_{stage}"
        counts = self.once_counts if stage == "W" else self.counts
        counts[sem] = counts.get(sem, 0) + add
        after = [d for a in after for d in (a if isinstance(a, list) else [a])]
        self.queues.setdefault(engine, []).append((after, make, sem, add, self.LEAD[stage], apart))
        return Done(sem, self.LEAD[stage], counts[sem])

    def dma(self, engine, stage, name, make, after=()):
        return self.step(engine, stage, make, after, f"dma_{name}", 16)

    def emit(self, eng, queue, sems, j, looped, spare=None):
        passed = {}
        for after, make, sem, add, lead, apart in queue:
            waits = 0
            for d in after:
                if d is None:
                    continue
                if d.lead is None:
                    if not looped and passed.get((d.sem, None), 0) < d.count:
                        passed[d.sem, None] = d.count
                        eng.wait_ge(sems[d.sem], d.count)
                    continue
                if not looped and j + d.lead < 0:
                    continue
                k = self.per_batch[d.sem]
                count = k if d.count == END else d.count
                if passed.get((d.sem, d.lead), 0) >= count:
                    continue
                passed[d.sem, d.lead] = count
                assert not looped or d.lead >= 0, d.sem
                eng.wait_ge(sems[d.sem], j * k + (d.lead * k + count))
                waits += 1
            if apart and looped and waits:
                eng.memset(spare, 0.0)
            make(eng, None if lead is None else j + lead).then_inc(sems[sem], add)


class Regions:

    def __init__(self, space):
        self.space, self.order = space, list(range(len(space)))
        self.last = [[] for _ in space]

    def start(self):
        self.order.sort()
        self.last = [[d if d.lead is None else Done(d.sem, d.lead - 1, d.count) for d in last] for last in self.last]


def layer_norm(plan, stage, x, out, stats, moments, rstd, half, after, free):
    def statistics(v, b):
        for n in range(ST):
            last = v.bn_stats(stats[:, n, :], x[:, n, :])
        return last

    def aggregate(v, b):
        for n in range(ST):
            last = v.bn_aggr(moments[:, n, :], stats[:, n, :])
        return last

    def normalise(v, b):
        for n in range(ST):
            last = v.tensor_scalar(out[:, n, :], x[:, n, :], moments[:, n, 0:1], rstd[:, n:n + 1],
                                   ALU.subtract, ALU.mult)
        return last

    t = plan.step("vector", stage, statistics, after)
    t = plan.step("vector", stage, aggregate, [t], apart=True)
    t = plan.step("vector", stage, lambda v, b: v.tensor_scalar(
        rstd[:, :], moments[:, :, 1], EPS, None, ALU.add), [t])
    t = plan.step("gpsimd", stage, lambda g, b: g.tensor_tensor(
        rstd[:, :], rstd[:, :], half[:, :], ALU.pow), [t, plan.once("minus half")])
    return plan.step("vector", stage, normalise, [t, *free])


def transpose_tiles(plan, stage, dst, src, ident, after):
    def make(pe, b):
        for n in range(ST):
            last = pe.transpose(dst[:, n * P:(n + 1) * P], src[:, n, :], ident[:, :])
        return last
    return plan.step("tensor", stage, make, [*after, plan.once("ident")])


def three_passes(pe, out, w_hi, w_lo, x_hi, x_lo, stop=True):
    pe.matmul(out, w_hi, x_hi, start=True, stop=False)
    pe.matmul(out, w_hi, x_lo, start=False, stop=False)
    return pe.matmul(out, w_lo, x_hi, start=False, stop=stop)


def f32(ap):
    return ap.bitcast(F32)


def build(nc, x, ctx_t, mask, attn_w, xq, xk, xv, xo, xbias, bo, w_router, w1, b1, w2, b2, out):
    stack = ExitStack()
    with stack:
        def sb(name, shape, dt=F32, at=stack):
            return at.enter_context(nc.sbuf_tensor(name, shape, dt))

        def psum(name, shape):
            return stack.enter_context(nc.psum_tensor(name, shape, F32))

        def dram(name, shape, dt):
            return nc.dram_tensor(name, shape, dt, kind="Internal").ap()

        a_all = dram("a_all", [NB, P, NX * T2], F32)
        u_all = dram("u_all", [NB, P, NPAIR * D], F32)
        r_all = dram("r_all", [NB, NX * T2], F32)
        parts_dram = dram("parts_dram", [3 * NPIECE - 1, P, S], BF16)

        big = [psum(f"big{n}", [P, 2 * 512]) for n in range(3)]
        small = [psum(f"small{n}", [P, 512]) for n in range(2)]

        ident = sb("ident", [P, P])
        minus_half = sb("minus_half", [P, ST])
        euler = sb("euler", [P, ST])
        spare = sb("spare", [1, 1])
        iota8 = sb("iota8", [P, NE])
        iota_i = sb("iota_i", [P, NE], I32)
        wqk_hi = sb("wqk_hi", [P, 2, P], F32R)
        wqk_lo = sb("wqk_lo", [P, 2, P], F32R)
        wv_wo = sb("wv_wo", [P, 2, P])
        bo_all = sb("bo_all", [P, D])
        wr = sb("wr", [P, NE])
        w1_hi = sb("w1_hi", [P, NE, FF], F32R)
        w1_lo = sb("w1_lo", [P, NE, FF], F32R)
        w2_sb = sb("w2_sb", [P, NE, FB, D])
        b1_sb = sb("b1_sb", [P, NE * FB])
        b2_sb = sb("b2_sb", [NE, D])

        main(nc, sb, big, small, locals())


def made_once(plan, sb, take, free_up, ones, twos, buffers, g):
    ident, w1_hi, w1_lo, w2_sb = g["ident"], g["w1_hi"], g["w1_lo"], g["w2_sb"]

    flat_w2 = w2_sb[:, :, :, :].rearrange("p e f d -> p (e f d)")
    weights = {n: flat_w2[:, k * NPAIR * D:(k + 1) * NPAIR * D].rearrange("p (q d) -> p q d", d=D)
               for k, n in enumerate(("xq", "xk", "xv", "xo"))}
    half_of = lambda t, k: t[:, k * (NE // 2):(k + 1) * (NE // 2), :].rearrange("p a b -> p (a b)")
    gt_hi, gt_lo = half_of(w1_hi, 0), half_of(w1_hi, 1)
    hh_hi, hh_lo = half_of(w1_lo, 0), half_of(w1_lo, 1)
    ctx, ctx_hi, ctx_lo = sb("ctx", [P, NB * T2]), sb("ctx_hi", [P, NB * T2], F32R), sb("ctx_lo", [P, NB * T2], F32R)
    wqk_raw, w1_raw = sb("wqk_raw", [P, 2, P]), sb("w1_raw", [P, NE // 2, FF])
    xb = sb("xb_sb", [P, 3, NPAIR])
    spread = [sb(f"spread_{n}", [P, NPAIR * (NX + 2)]) for n in ("bq", "bk")]
    bv_cols = sb("bv_cols", [P, NPAIR, P])
    bqk, bqk_sum = sb("bqk", [P, NPAIR, NX]), sb("bqk_sum", [P, NX])
    ones_col = sb("ones_col", [P, 1])
    vec_rows = sb("vec_rows", [NX, 2, D])
    vecs = sb("vecs", [P, 2, NX])
    beta = sb("beta", [NX, 1])
    u_bias = sb("u_bias", [P, 2, NPAIR * D])
    r_f = w1_raw[0:NX, 0:2, :].rearrange("h a n -> h (a n)")

    def load(name, dst, src, after=()):
        return plan.name(name, plan.dma("sync", "W", name, lambda e, b: e.dma_start(dst, src), after))

    W = lambda engine, make, after=(): plan.step(engine, "W", make, after)

    got_wqk = load("wqk", wqk_raw[:, :, :], g["attn_w"][:, 0:2, :])
    yield "load0"
    got_xk = load("xk", weights["xk"], g["xk"])
    got_xq = load("xq", weights["xq"], g["xq"])
    got_xb = load("xbias", xb[:, :, :], g["xbias"])
    got_ctx = load("ctx", ctx[:, :], g["ctx_t"])
    got_xv = load("xv", weights["xv"], g["xv"])
    got_xo = load("xo", weights["xo"], g["xo"])
    load("wv_wo", g["wv_wo"][:, :, :], g["attn_w"][:, 2:4, :])
    load("bo_in", g["bo_all"][:, :], g["bo"].partition_broadcast(P))
    load("wr_in", g["wr"][:, :], g["w_router"])
    load("b1_in", g["b1_sb"][:, :], g["b1"])
    load("b2_in", g["b2_sb"][:, :], g["b2"])
    yield "load1"

    t = W("gpsimd", lambda e, b: e.memset(ident[:, :], 0.0))
    got_ident = plan.name("ident", W("gpsimd", lambda e, b: e.affine_select(
        out=ident[:, :], in_=ident[:, :], compare_op=ALU.not_equal, fill=1.0, base=0,
        pattern=[[-1, P]], channel_multiplier=1), [t]))
    t = W("gpsimd", lambda e, b: e.iota(g["iota_i"][:, :], pattern=[[1, NE]], base=0, channel_multiplier=0))
    t_z = [W("gpsimd", lambda e, b, k=k: e.memset(spread[k][:, :], 0.0)) for k in range(2)]
    plan.name("minus half", W("vector", lambda e, b: e.memset(g["minus_half"][:, :], -0.5)))
    W("vector", lambda e, b: e.memset(g["euler"][:, :], float(np.e)))
    got_ones = W("vector", lambda e, b: e.memset(ones_col[:, :], 1.0))
    W("vector", lambda e, b: e.tensor_copy(g["iota8"][:, :], g["iota_i"][:, :]), [t])
    yield "const"

    t = W("vector", lambda v, b: v.tensor_copy(g["wqk_hi"][:, :, :], wqk_raw[:, :, :]), [got_wqk])
    plan.name("wqk parts", W("vector", lambda v, b: v.tensor_tensor(
        g["wqk_lo"][:, :, :], wqk_raw[:, :, :], f32(g["wqk_hi"][:, :, :]), ALU.subtract), [t]))
    yield "wqk"
    t = W("vector", lambda v, b: v.tensor_copy(ctx_hi[:, :], ctx[:, :]), [got_ctx])
    got_ctx = W("vector", lambda v, b: v.tensor_tensor(ctx_lo[:, :], ctx[:, :], f32(ctx_hi[:, :]), ALU.subtract), [t])
    yield "ctx"

    def fold(q0, left, right, hi, lo, after):
        n, ps, free = take(twos)

        def make(pe, b):
            for k in range(4):
                for par in range(2):
                    rows = slice(par * DX, (par + 1) * DX)
                    last = pe.matmul(ps[:, par * 512 + k * D:par * 512 + (k + 1) * D], left[rows, q0 + k, :],
                                     right[rows, q0 + k, :], start=True, stop=True)
            return last
        by_parity = lambda a: a.rearrange("p (a n) -> p a n", a=2)
        hi, lo = (by_parity(a)[:, :, q0 * D:(q0 + 4) * D] for a in (hi, lo))
        t = W("tensor", make, [*after, free])
        t = W("vector", lambda v, b: v.tensor_copy(hi, by_parity(ps[:, :])), [t])
        t = W("vector", lambda v, b: v.tensor_tensor(lo, by_parity(ps[:, :]), f32(hi), ALU.subtract), [t])
        free_up(twos, n, t)
        return t

    got_g, got_h = [], []
    for i in range(2):
        got_g.append(fold(4 * i, weights["xk"], weights["xq"], gt_hi, gt_lo, [got_xk, got_xq]))
        yield f"fold{i}"

    t_s = []
    for k in range(2):
        for par in range(2):
            rows = slice(par * DX, (par + 1) * DX)
            t_s.append(W("vector", lambda v, b, k=k, par=par, rows=rows: v.tensor_copy(
                spread[k][rows, :].rearrange("p (q w) -> p q w", w=NX + 2)[:, :, par], xb[rows, k, :]),
                [got_xb, t_z[k]]))
    n, ps, free = take(ones)

    def vectors(pe, b, ps=ps):
        for k, (x, bias) in enumerate((("xq", 1), ("xk", 0))):
            for q in range(NPAIR):
                last = pe.matmul(ps[0:NX, k * D:(k + 1) * D], spread[bias][:, q * NX:(q + 1) * NX],
                                 weights[x][:, q, :], start=(q == 0), stop=(q == NPAIR - 1))
        return last
    t = W("tensor", vectors, [*t_s, got_xq, got_xk, free])
    t = W("vector", lambda v, b, ps=ps: v.tensor_copy(
        vec_rows[:, :, :].rearrange("h k d -> h (k d)"), ps[0:NX, 0:2 * D]), [t])
    free_up(ones, n, t)
    n, ps, free = take(ones)

    def turn_vectors(pe, b, ps=ps):
        for k in range(2):
            last = pe.transpose(ps[:, k * NX:(k + 1) * NX], vec_rows[:, k, :], ident[0:NX, 0:NX])
        return last
    t = W("tensor", turn_vectors, [t, got_ident, free])
    got_vecs = W("vector", lambda v, b, ps=ps: v.tensor_copy(
        vecs[:, :, :].rearrange("p k h -> p (k h)"), ps[:, 0:2 * NX]), [t])
    free_up(ones, n, got_vecs)
    yield "vectors"

    t = W("vector", lambda v, b: v.tensor_tensor(
        bqk[:, :, :], spread[0][:, 0:NPAIR * NX].rearrange("p (q h) -> p q h", h=NX),
        xb[:, 1, :].unsqueeze(2).to_broadcast([P, NPAIR, NX]), ALU.mult), [*t_s])
    t = W("vector", lambda v, b: v.tensor_reduce(
        bqk_sum[:, :], bqk[:, :, :].rearrange("p q h -> p h q"), AX.X, ALU.add), [t])
    n, ps, free = take(ones)
    t = W("tensor", lambda pe, b, ps=ps: pe.matmul(
        ps[0:NX, 0:1], bqk_sum[:, :], ones_col[:, :], start=True, stop=True), [t, got_ones, free])
    got_beta = W("vector", lambda v, b, ps=ps: v.tensor_copy(beta[:, :], ps[0:NX, 0:1]), [t])
    free_up(ones, n, got_beta)
    for half in range(2):
        cols = slice(half * 512, half * 512 + 512)
        n, ps, free = take(ones)
        t = W("tensor", lambda pe, b, ps=ps, cols=cols: pe.matmul(
            ps[0:NX, :], vecs[:, 1, :], ctx[:, cols], start=True, stop=True), [got_vecs, got_ctx, free])
        t = W("vector", lambda v, b, ps=ps, cols=cols: v.tensor_scalar(
            r_f[:, cols], ps[0:NX, :], beta[:, 0:1], None, ALU.add), [t, got_beta])
        free_up(ones, n, t)
    plan.name("r stored", plan.dma("sync", "W", "r_out", lambda e, b: e.dma_start(
        g["r_all"].rearrange("b (h t) -> h b t", t=T2), r_f[:, :].rearrange("h (b t) -> h b t", b=NB)), [t]))
    yield "rows"

    for i in range(2):
        got_h.append(fold(4 * i, weights["xv"], weights["xo"], hh_hi, hh_lo, [got_xv, got_xo]))
        yield f"fold_v{i}"
    t_bv = W("vector", lambda v, b: v.tensor_copy(
        bv_cols[:, :, :], xb[:, 2, :].unsqueeze(2).to_broadcast([P, NPAIR, P])), [got_xb])
    got_ub = []
    for par in range(2):
        n, ps, free = take(twos)

        def value_bias(pe, b, ps=ps, rows=slice(par * DX, (par + 1) * DX)):
            for q in range(NPAIR):
                last = pe.matmul(ps[:, q * D:(q + 1) * D], bv_cols[rows, q, :], weights["xo"][rows, q, :],
                                 start=True, stop=True)
            return last
        t = folded = W("tensor", value_bias, [t_bv, got_xo, free])
        t = W("vector", lambda v, b, ps=ps, par=par: v.tensor_copy(u_bias[:, par, :], ps[:, :]), [t])
        free_up(twos, n, t)
        got_ub.append(t)
    yield "bias"

    GB = 4
    stored = [None] * len(buffers)
    fill = 0
    for g0 in range(0, NB, GB):
        k0 = fill % len(buffers)
        fill += 1
        buf, wait = buffers[k0], stored[k0]
        for h0 in range(0, NX, 4):
            n, ps, free = take(twos)

            def key_side(pe, b, h0=h0, g0=g0, ps=ps):
                rows = slice(g0 * T2, (g0 + GB) * T2)
                for k in range(4):
                    at = (h0 + k) % 2 * NPAIR + (h0 + k) // 2
                    cols = slice(at * D, (at + 1) * D)
                    last = three_passes(pe, ps[:, k * GB * T2:(k + 1) * GB * T2], gt_hi[:, cols], gt_lo[:, cols],
                                        ctx_hi[:, rows], ctx_lo[:, rows])
                return last
            t = through = W("tensor", key_side, [*got_g, got_ctx, free])

            def keep(k, h0=h0, buf=buf, ps=ps):
                return (buf[:, :, (h0 + k) * T2:(h0 + k + 1) * T2],
                        ps[:, k * GB * T2:(k + 1) * GB * T2].rearrange("p (b t) -> p b t", t=T2),
                        vecs[:, 0, h0 + k:h0 + k + 1])

            def keep_scalar(a, b, keep=keep):
                for k in range(2):
                    to, of, bias = keep(k)
                    last = a.activation(to, of, ACT.Identity, bias=bias)
                return last

            def keep_vector(v, b, keep=keep):
                for k in range(2, 4):
                    to, of, bias = keep(k)
                    last = v.tensor_scalar(to, of, bias, None, ALU.add)
                return last
            t1 = W("scalar", keep_scalar, [t, got_vecs, wait])
            t2 = W("vector", keep_vector, [t, got_vecs, wait])
            free_up(twos, n, [t1, t2])
            yield f"key{g0 // GB}{h0 // 4}"
        stored[k0] = plan.dma("sync", "W", f"a_out{g0 // GB}", lambda e, b, g0=g0, buf=buf: e.dma_start(
            g["a_all"][g0:g0 + GB].rearrange("b p n -> p b n"), buf[:, :, :]), [t1, t2])
        plan.name(f"a stored{g0 // GB}", stored[k0])

        k0 = fill % len(buffers)
        fill += 1
        buf, wait = buffers[k0], stored[k0]
        for k in range(GB):
            b0, par = g0 + k // 2 * 2, k % 2
            n, ps, free = take(twos)

            def value_side(pe, b, b0=b0, par=par, ps=ps):
                rows = slice(b0 * T2, (b0 + 2) * T2)
                for c in range(2):
                    cols = slice((2 * par + c) * 512, (2 * par + c + 1) * 512)
                    last = three_passes(pe, ps[:, c * 512:(c + 1) * 512], ctx_hi[:, rows], ctx_lo[:, rows],
                                        hh_hi[:, cols], hh_lo[:, cols])
                return last
            t = through = W("tensor", value_side, [*got_h, got_ctx, free])
            t = W("vector", lambda v, b, k=k, par=par, buf=buf, ps=ps: v.tensor_tensor(
                buf[:, k, :], ps[:, :], u_bias[:, par, :], ALU.add), [t, *got_ub, wait])
            free_up(twos, n, t)
            if par:
                for c in range(2):
                    stored[k0] = plan.dma("sync", "W", f"u_out{g0 // GB}", lambda e, b, b0=b0, c=c, k=k, buf=buf:
                                          e.dma_start(g["u_all"][b0 + c].rearrange("(a t) n -> t a n", a=2),
                                                      buf[c * T2:(c + 1) * T2, k - 1:k + 1, :]), [t])
            yield f"value{g0 + k}"
        plan.name(f"u stored{g0 // GB}", stored[k0])
        yield f"store{g0 // GB}"
    load("w2_in", w2_sb[:, :, :, :], g["w2"], [folded, *got_g, *got_h])
    got_w1 = load("w1_a", w1_raw[:, :, :], g["w1"][:, 0:NE // 2, :], [plan.once("r stored")])
    yield "experts"
    for e0 in range(NE):
        raw = w1_raw[:, e0 % (NE // 2), :]
        t = W("gpsimd", lambda e, b, e0=e0, raw=raw: e.tensor_copy(w1_hi[:, e0, :], raw), [got_w1, through])
        t = W("vector", lambda v, b, e0=e0, raw=raw: v.tensor_tensor(
            w1_lo[:, e0, :], raw, f32(w1_hi[:, e0, :]), ALU.subtract), [t])
        yield f"w1_{e0}"
        if e0 == NE // 2 - 1:
            got_w1 = load("w1_b", w1_raw[:, :, :], g["w1"][:, NE // 2:, :], [t])
            yield "w1_b"


def main(nc, sb, big, small, g):
    ident, minus_half = g["ident"], g["minus_half"]

    x_in = sb("x_in", [P, ST, D])
    x_keep = sb("x_keep", [P, ST, D])
    xn = sb("xn", [P, ST, D])
    stats_a, moments_a, rstd_a = sb("stats_a", [P, ST, 6]), sb("moments_a", [P, ST, 2]), sb("rstd_a", [P, ST])
    xt, xt_hi, xt_lo = sb("xt", [P, S]), sb("xt_hi", [P, S], F32R), sb("xt_lo", [P, S], F32R)
    parts = sb("parts", [P, NPIECE, 2, S], BF16)
    rest = sb("rest", [P, 2 * S])
    v_cols = sb("v_cols", [P, ST, NH, 32])
    q_stack = sb("q_stack", [P, NH, S], BF16)
    k_stack = sb("k_stack", [P, NH, S], BF16)
    max_a = sb("max_a", [P, ST, NH])
    max_parts = sb("max_parts", [NH, NPIECE, S], BF16)
    max_rest = sb("max_rest", [NH, S])
    NPROB = 3
    probs = [sb(f"probs{n}", [P, 4, S]) for n in range(NPROB)]
    o_cols = sb("o_cols", [P, 4, S])
    rec_a = sb("rec_a", [P, ST, NH])
    attn = sb("attn", [P, ST, NH, DK])
    attn_t = sb("attn_t", [P, S])
    x2, x2_bo, xn2 = sb("x2", [P, ST, D]), sb("x2_bo", [P, ST, D]), sb("xn2", [P, ST, D])
    x2t_hi, x2t_lo = sb("x2t_hi", [P, S], F32R), sb("x2t_lo", [P, S], F32R)
    stats_b, moments_b, rstd_b = sb("stats_b", [P, ST, 6]), sb("moments_b", [P, ST, 2]), sb("rstd_b", [P, ST])
    buffers = [sb(f"buffer{n}", [P, 4, 1024]) for n in range(NBUF)]
    a_b, u_b = buffers[0][:, 0, :], buffers[0][:, 1, :].rearrange("p (q d) -> p q d", d=D)
    hidden = [buffers[0][:, n, :].rearrange("p (f s) -> p f s", f=FB) for n in (2, 3)]
    s_b = buffers[1][:, 0:2, :].rearrange("p m (h t) -> p m h t", h=NX)
    p_t = buffers[1][:, 2:4, :].rearrange("p a n -> p (a n)").rearrange("p (q s) -> p q s", q=NPAIR)
    a_hi, a_lo = sb("a_hi", [P, NX * T2], F32R), sb("a_lo", [P, NX * T2], F32R)
    r_b = sb("r_b", [P, NX, T2])
    shift = sb("shift", [P, ST, NX, T2])
    mask_i = sb("mask_i", [P, ST, T2], I32)
    mask_neg = sb("mask_neg", [P, ST, T2])
    any_b = sb("any_b", [P, ST])
    max_b, rec_b = sb("max_b", [P, ST, NX]), sb("rec_b", [P, ST, NX])
    x3, xn3, x3t = sb("x3", [P, ST, D]), sb("xn3", [P, ST, D]), sb("x3t", [P, S])
    x3_hi, x3_lo = sb("x3_hi", [P, S], F32R), sb("x3_lo", [P, S], F32R)
    logits, top_v = sb("logits", [P, ST, NE]), sb("top_v", [P, ST, NE])
    top_i, top_if = sb("top_i", [P, ST, NE], U32), sb("top_if", [P, ST, 2])
    gate = sb("gate", [P, 4, ST])
    cw2 = sb("cw2", [P, 2, ST, NE])
    cw = sb("cw", [P, ST, NE])
    cw_t = sb("cw_t", [NE, S])
    acc = sb("acc", [P, ST, D])

    plan = Plan()
    ones, twos = Regions(small), Regions(big)
    made = {}

    def sb_once(name, shape, dt=F32):
        if name not in made:
            made[name] = sb(name, shape, dt)
        return made[name]

    def take(regions, n=None):
        if n is None:
            n = regions.order[0]
        regions.order.remove(n)
        return n, regions.space[n], regions.last[n]

    def free_up(regions, n, done):
        regions.order.append(n)
        regions.last[n] = done if isinstance(done, list) else [done]

    def iteration(has, order, once=None):
        plan.start()
        for regions in (ones, twos):
            regions.start()
        last_of = {}

        def earlier(point, stage):
            assert point in last_of or stage not in has, point
            return last_of.get(point)

        def take_small():
            return take(ones)

        def free_small(n, done):
            free_up(ones, n, done)

        def stage_l():
            L = lambda engine, make, after=(): plan.step(engine, "L", make, after)
            got_x = plan.dma("sync", "L", "x", lambda e, b: e.dma_start(
                x_in[:, :, :], g["x"][b].rearrange("(n p) d -> p n d", p=P)), [plan.before("x normalised")])
            yield "load"
            t_n = layer_norm(plan, "L", x_in, xn, stats_a, moments_a, rstd_a, minus_half, [got_x], [])
            plan.name("x normalised", t_n)
            yield "norm"
            n, ps_t, free = take_small()
            t = transpose_tiles(plan, "L", ps_t, xn, ident, [t_n, free])
            t_xt = plan.name("xt", L("scalar", lambda a, b: a.activation(xt[:, :], ps_t[:, 0:S], ACT.Copy),
                                     [t, earlier("values read", "A")]))
            t_hi = L("vector", lambda v, b: v.tensor_copy(xt_hi[:, :], xt[:, :]), [t_xt])
            t_lo = L("vector", lambda v, b: v.tensor_tensor(xt_lo[:, :], xt[:, :], f32(xt_hi[:, :]),
                                                           ALU.subtract), [t_hi])
            free_small(n, t_xt)
            yield "turn"
            n, ps_qk, free = take_small()

            def project(pe, b):
                for c in range(2):
                    last = three_passes(pe, ps_qk[:, c * S:(c + 1) * S], g["wqk_hi"][:, c, :], g["wqk_lo"][:, c, :],
                                        xt_hi[:, :], xt_lo[:, :])
                return last
            t = L("tensor", project, [t_lo, free, plan.once("wqk parts")])
            t = L("vector", lambda v, b: v.tensor_copy(
                parts[:, 0, :, :].rearrange("p c s -> p (c s)"), ps_qk[:, :]), [t, plan.before("parts out")])
            t = L("vector", lambda v, b: v.tensor_tensor(
                rest[:, :], ps_qk[:, :], parts[:, 0, :, :].rearrange("p c s -> p (c s)"), ALU.subtract), [t])
            free_small(n, t)
            yield "qk"
            t = L("vector", lambda v, b: v.tensor_copy(
                parts[:, 1, :, :].rearrange("p c s -> p (c s)"), rest[:, :]), [t])
            t = L("vector", lambda v, b: v.tensor_tensor(
                parts[:, 2, :, :].rearrange("p c s -> p (c s)"), rest[:, :],
                parts[:, 1, :, :].rearrange("p c s -> p (c s)"), ALU.subtract), [t])
            for to, c, n in ((0, 0, NPIECE), (NPIECE, 0, NPIECE - 1), (2 * NPIECE - 1, 1, NPIECE)):
                t_w = plan.dma("sync", "L", "parts_out", lambda e, b, to=to, c=c, n=n: e.dma_start(
                    g["parts_dram"][to:to + n].rearrange("k p s -> p k s"), parts[:, 0:n, c, :]),
                    [t, earlier("stacked", "A")])
            plan.name("parts out", t_w)
            yield "parts"

        def stage_a():
            A = lambda engine, make, after=(): plan.step(engine, "A", make, after)
            prev = lambda engine: Done(f"{engine}_A", 1, END)
            t_w = plan.before("parts out")
            for r in range(NPIECE):
                for stack, first in ((q_stack, r), (k_stack, 2 * NPIECE - 1)):
                    t_st = plan.dma("sync", "A", "stacks", lambda e, b, r=r, stack=stack, first=first: e.dma_start(
                        stack[r * NPIECE * DK:(r + 1) * NPIECE * DK, :, :],
                        g["parts_dram"][first:first + NPIECE].rearrange("k (d h) s -> (k d) h s", d=DK)),
                        [t_w, plan.before("keys")])
            last_of["stacked"] = t_st
            yield "stacks"
            n, ps_v, free = take_small()

            def values(pe, b):
                for m in range(ST):
                    last = pe.matmul(ps_v[:, m * P:(m + 1) * P], xt[:, m * P:(m + 1) * P], g["wv_wo"][:, 0, :],
                                     start=True, stop=True)
                return last
            t = last_of["values read"] = A("tensor", values, [plan.before("xt"), free, plan.once("wv_wo")])
            t_v = A("scalar", lambda a, b: a.activation(
                v_cols[:, :, :, 0:DK], ps_v[:, 0:ST * P].rearrange("p (m h d) -> p m h d", m=ST, h=NH),
                ACT.Copy), [t, prev("tensor")])
            free_small(n, t_v)
            yield "v"
            for m in range(ST):
                for h0 in range(0, NH, 4):
                    n, ps, free = take(twos)

                    def scores(pe, b, m=m, h0=h0, ps=ps):
                        for h in range(h0, h0 + 4):
                            last = pe.matmul(ps[:, (h - h0) * S:(h - h0 + 1) * S],
                                             q_stack[0:ROWS, h, m * P:(m + 1) * P], k_stack[0:ROWS, h, :],
                                             start=True, stop=True)
                        return last
                    t = A("tensor", scores, [t_st, free])
                    t_mx = A("vector", lambda v, b, m=m, h0=h0, ps=ps: v.tensor_reduce(
                        max_a[:, m, h0:h0 + 4], ps[:, :].rearrange("p (h t) -> p h t", h=4),
                        AX.X, ALU.max), [t])
                    free_up(twos, n, t_mx)
                    yield f"max{m * 4 + h0 // 4}"
            n, ps_m, free = take_small()

            def turn_max(pe, b):
                for m in range(ST):
                    last = pe.transpose(ps_m[0:NH, m * P:(m + 1) * P], max_a[:, m, :], ident[:, :])
                return last
            t = A("tensor", turn_max, [t_mx, free])
            t = A("vector", lambda v, b: v.tensor_scalar(
                max_parts[:, 0, :], ps_m[0:NH, 0:S], -1.0, None, ALU.mult), [t])
            t = A("vector", lambda v, b: v.scalar_tensor_tensor(
                max_rest[:, :], ps_m[0:NH, 0:S], -1.0, max_parts[:, 0, :], ALU.mult, ALU.subtract), [t])
            free_small(n, t)
            t = A("vector", lambda v, b: v.tensor_copy(max_parts[:, 1, :], max_rest[:, :]), [t])
            t = A("vector", lambda v, b: v.tensor_tensor(
                max_parts[:, 2, :], max_rest[:, :], max_parts[:, 1, :], ALU.subtract), [t])
            for k in range(NPIECE):
                t_m = plan.dma("sync", "A", "max_rows", lambda e, b, k=k: e.dma_start(
                    q_stack[ROWS + k:ROWS + k + 1, :, :], max_parts[:, k, :]), [t])
            yield "turn_max"
            t_exp, t_s = [None] * 8, [None] * 8
            t_pv = [None] * 8

            def by_key(u):
                h0, m = 4 * (u // ST), u % ST
                n, ps, free = take(twos)

                def make(pe, b):
                    for h in range(h0, h0 + 4):
                        last = pe.matmul(ps[:, (h - h0) * S:(h - h0 + 1) * S],
                                         k_stack[0:ROWS + NPIECE, h, m * P:(m + 1) * P],
                                         q_stack[0:ROWS + NPIECE, h, :], start=True, stop=True)
                    return last
                t_s[u] = A("tensor", make, [t_m, free])
                if u == 7:
                    plan.name("keys", t_s[u])
                t_exp[u] = A("scalar", lambda a, b: a.activation(
                    probs[u % NPROB][:, :, :].rearrange("p h s -> p (h s)"), ps[:, :], ACT.Exp, scale=SCALE_A),
                    [t_s[u], t_pv[u - NPROB] if u >= NPROB else None])
                free_up(twos, n, t_exp[u])

            def times_v(u, sums, free):
                h0, m = 4 * (u // ST), u % ST

                def make(pe, b):
                    for h in range(h0, h0 + 4):
                        j = h - h0
                        last = pe.matmul(sums[32 * j:32 * j + 32, (h0 // 4) * S:(h0 // 4 + 1) * S],
                                         v_cols[:, m, h, :], probs[u % NPROB][:, j, :],
                                         start=(m == 0), stop=(m == ST - 1))
                    return last
                t_pv[u] = A("tensor", make, [t_exp[u], t_v, free])

            by_key(0)
            yield "key0"
            by_key(1)
            yield "key1"
            n, sums, free = take(twos, SUMS)
            for u in range(8):
                times_v(u, sums, free)
                yield f"values{u}"
                if u + 2 < 8:
                    by_key(u + 2)
                    yield f"key{u + 2}"

        def stage_m():
            M = lambda engine, make, after=(): plan.step(engine, "M", make, after)
            stored = [plan.once(f"{x} stored{k}") for x in "au" for k in range(4)]
            got_a = plan.dma("sync", "M", "a_in", lambda e, b: e.dma_start(a_b, g["a_all"][b]),
                             [plan.before("a parts"), *stored])
            got_r = plan.dma("sync", "M", "r_in", lambda e, b: e.dma_start(
                r_b[:, :, :].rearrange("p h t -> p (h t)"), g["r_all"][b].partition_broadcast(P)),
                [plan.before("shift"), plan.once("r stored")])
            got_mask = plan.dma("sync", "M", "mask_in", lambda e, b: e.dma_start(
                mask_i[:, :, :], g["mask"][b].rearrange("(n p) t -> p n t", p=P)), [plan.before("mask")])
            yield "load"
            t_mk = M("vector", lambda v, b: v.tensor_scalar(
                mask_neg[:, :, :], mask_i[:, :, :], 0.0, MASKED / SCALE_B, ALU.is_equal, ALU.mult), [got_mask])
            plan.name("mask", t_mk)
            t = M("vector", lambda v, b: v.tensor_reduce(any_b[:, :], mask_neg[:, :, :], AX.X, ALU.max), [t_mk])
            last_of["any"] = M("vector", lambda v, b: v.tensor_scalar(
                any_b[:, :], any_b[:, :], 0.0, None, ALU.is_equal), [t])
            for m in range(ST):
                t_sh = M("gpsimd", lambda e, b, m=m: e.tensor_tensor(
                    shift[:, m, :, :], r_b[:, :, :], mask_neg[:, m, :].unsqueeze(1).to_broadcast([P, NX, T2]), ALU.add),
                    [t_mk, got_r, plan.before("masked")])
            last_of["shift"] = plan.name("shift", t_sh)
            yield "shift"
            t_ah = M("vector", lambda v, b: v.tensor_copy(a_hi[:, :], a_b), [got_a, plan.before("scores")])
            last_of["a parts"] = plan.name("a parts", M("gpsimd", lambda e, b: e.tensor_tensor(
                a_lo[:, :], a_b, f32(a_hi[:, :]), ALU.subtract), [t_ah, plan.before("scores")]))
            yield "a"

        def stage_b():
            B = lambda engine, make, after=(): plan.step(engine, "B", make, after)
            stored = [plan.once(f"{x} stored{k}") for x in "au" for k in range(4)]
            got_u = plan.dma("sync", "B", "u_in", lambda e, b: e.dma_start(
                u_b[:, :, :], g["u_all"][b].rearrange("p (q d) -> p q d", d=D)), [plan.before("times u"), *stored])
            got_x = plan.dma("sync", "B", "x_keep", lambda e, b: e.dma_start(
                x_keep[:, :, :], g["x"][b].rearrange("(n p) d -> p n d", p=P)), [plan.before("x2")])
            yield "load"
            t = B("scalar", lambda a, b: a.activation(
                o_cols[:, :, :].rearrange("p q s -> p (q s)"), big[SUMS][:, :], ACT.Copy), [Done("tensor_A", 1, END)])
            t_o = t
            free_up(twos, SUMS, t)
            yield "sums"
            for m in range(ST):
                n, ps, free = take_small()

                def turn(pe, b, ps=ps, m=m):
                    for q in range(4):
                        last = pe.transpose(ps[:, q * P:(q + 1) * P], o_cols[:, q, m * P:(m + 1) * P], ident[:, :])
                    return last
                t1 = B("tensor", turn, [t_o, free])
                cols = ps[:, :].rearrange("p (h w) -> p h w", w=32)
                t2 = B("vector", lambda v, b, m=m, cols=cols: v.reciprocal(rec_a[:, m, :], cols[:, :, DK]), [t1])
                t_at = B("vector", lambda v, b, m=m, cols=cols: v.tensor_tensor(
                    attn[:, m, :, :], cols[:, :, 0:DK], rec_a[:, m, :].unsqueeze(2).to_broadcast([P, NH, DK]),
                    ALU.mult), [t2])
                free_small(n, t_at)
            yield "normalise"
            n, ps1, free = take_small()
            t = transpose_tiles(plan, "B", ps1, attn[:, :, :, :].rearrange("p m h d -> p m (h d)"), ident,
                                [t_at, free])
            t = B("scalar", lambda a, b: a.activation(attn_t[:, :], ps1[:, 0:S], ACT.Copy), [t])
            free_small(n, t)
            yield "turn"
            n, ps2, free = take_small()

            def project(pe, b):
                for m in range(ST):
                    last = pe.matmul(ps2[:, m * P:(m + 1) * P], attn_t[:, m * P:(m + 1) * P], g["wv_wo"][:, 1, :],
                                     start=True, stop=True)
                return last
            t = B("tensor", project, [t, free])
            t = B("vector", lambda v, b: v.tensor_tensor(
                x2[:, :, :], ps2[:, 0:S].rearrange("p (m d) -> p m d", m=ST), x_keep[:, :, :], ALU.add),
                [t, got_x])
            plan.name("x2", t)
            free_small(n, t)
            t_bo = B("gpsimd", lambda e, b: e.tensor_tensor(
                x2_bo[:, :, :], x2[:, :, :], g["bo_all"][:, :].unsqueeze(1).to_broadcast([P, ST, D]), ALU.add),
                [t, plan.once("bo_in")])
            t_n = layer_norm(plan, "B", x2, xn2, stats_b, moments_b, rstd_b, minus_half, [t], [])
            yield "project"
            n, ps3, free = take_small()
            t = transpose_tiles(plan, "B", ps3, xn2, ident, [t_n, free])
            t = B("vector", lambda v, b: v.tensor_copy(x2t_hi[:, :], ps3[:, 0:S]), [t])
            t_xt = B("vector", lambda v, b: v.tensor_tensor(
                x2t_lo[:, :], ps3[:, 0:S], f32(x2t_hi[:, :]), ALU.subtract), [t])
            free_small(n, t_xt)
            yield "turn_x2"
            t_sub = [None] * ST
            for m in range(ST):
                n, ps, free = take(twos)

                def scores(pe, b, m=m, ps=ps):
                    for k in range(2):
                        cols = slice(k * 512, (k + 1) * 512)
                        last = three_passes(pe, ps[:, cols], x2t_hi[:, m * P:(m + 1) * P],
                                            x2t_lo[:, m * P:(m + 1) * P], a_hi[:, cols], a_lo[:, cols])
                    return last
                t = B("tensor", scores, [t_xt, earlier("a parts", "M"), free])
                plan.name("scores", t)
                t = B("vector", lambda v, b, m=m, ps=ps: v.tensor_tensor(
                    s_b[:, m, :, :], ps[:, :].rearrange("p (h t) -> p h t", h=NX),
                    shift[:, m, :, :], ALU.add), [t, earlier("shift", "M")])
                plan.name("masked", t)
                free_up(twos, n, t)
                t = B("vector", lambda v, b, m=m: v.tensor_reduce(
                    max_b[:, m, :], s_b[:, m, :, :], AX.X, ALU.max), [t])
                t_sub[m] = B("gpsimd", lambda e, b, m=m: e.tensor_tensor(
                    s_b[:, m, :, :], s_b[:, m, :, :], max_b[:, m, :].unsqueeze(2).to_broadcast([P, NX, T2]),
                    ALU.subtract), [t])
                yield f"scores{m}"
            t_p = [None] * ST
            for m in range(ST):
                t = B("scalar", lambda a, b, m=m: a.activation(
                    s_b[:, m, :, :], s_b[:, m, :, :], ACT.Exp, scale=SCALE_B), [t_sub[m]])
                t = B("vector", lambda v, b, m=m: v.tensor_reduce(
                    rec_b[:, m, :], s_b[:, m, :, :], AX.X, ALU.add), [t])
                t = B("vector", lambda v, b, m=m: v.reciprocal(rec_b[:, m, :], rec_b[:, m, :]), [t])
                t = B("vector", lambda v, b, m=m: v.tensor_scalar(
                    rec_b[:, m, :], rec_b[:, m, :], any_b[:, m:m + 1], None, ALU.mult), [t, earlier("any", "M")])
                t_p[m] = B("vector", lambda v, b, m=m: v.tensor_tensor(
                    s_b[:, m, :, :], s_b[:, m, :, :], rec_b[:, m, :].unsqueeze(2).to_broadcast([P, NX, T2]),
                    ALU.mult), [t])
                yield f"exp{m}"
            t_pt = []
            for m in range(ST):
                for q0 in range(0, NPAIR, 4):
                    n, ps, free = take_small()

                    def turn(pe, b, ps=ps, m=m, q0=q0):
                        for q in range(4):
                            last = pe.transpose(
                                ps[:, q * P:(q + 1) * P],
                                s_b[:, m, 2 * (q0 + q):2 * (q0 + q) + 2, :].rearrange("p h t -> p (h t)"), ident[:, :])
                        return last
                    t = B("tensor", turn, [t_p[m], free])
                    to = p_t[:, q0:q0 + 4, m * P:(m + 1) * P]
                    src = ps[:, :].rearrange("p (q s) -> p q s", q=4)
                    t = B("vector", lambda v, b, to=to, src=src: v.tensor_copy(to, src), [t])
                    free_small(n, t)
                    t_pt.append(t)
                    yield f"turn_p{m}{q0 // 4}"
            n, ps4, free = take_small()

            def times_u(pe, b):
                for m in range(ST):
                    for q in range(NPAIR):
                        last = pe.matmul(ps4[:, m * P:(m + 1) * P], p_t[:, q, m * P:(m + 1) * P], u_b[:, q, :],
                                         start=(q == 0), stop=(q == NPAIR - 1))
                return last
            t = B("tensor", times_u, [*t_pt, got_u, free])
            yield "times_u"
            plan.name("times u", t)
            t_x3 = B("vector", lambda v, b: v.tensor_tensor(
                x3[:, :, :], ps4[:, 0:S].rearrange("p (m d) -> p m d", m=ST), x2_bo[:, :, :], ALU.add),
                [t, t_bo, earlier("x3 read", "C")])
            plan.name("x3", t_x3)
            free_small(n, t_x3)
            t_n = layer_norm(plan, "B", x3, xn3, stats_b, moments_b, rstd_b, minus_half, [t_x3], [])
            yield "norm3"
            n, ps5, free = take_small()
            t = transpose_tiles(plan, "B", ps5, xn3, ident, [t_n, free])
            t_xt = plan.name("x3t", B("scalar", lambda a, b: a.activation(x3t[:, :], ps5[:, 0:S], ACT.Copy),
                                      [t, earlier("routed", "C")]))
            free_small(n, t_xt)
            t = B("vector", lambda v, b: v.tensor_copy(x3_hi[:, :], x3t[:, :]), [t_xt, earlier("up", "C")])
            plan.name("x3 parts", B("vector", lambda v, b: v.tensor_tensor(
                x3_lo[:, :], x3t[:, :], f32(x3_hi[:, :]), ALU.subtract), [t, earlier("stored", "C")]))
            yield "turn_x3"

        def stage_c():
            C = lambda engine, make, after=(): plan.step(engine, "C", make, after)
            parts_3, got_x3t, got_x3 = plan.before("x3 parts"), plan.before("x3t"), plan.before("x3")
            t_up, t_gelu, t_down = {}, {}, {}

            def up(e0):
                n, ps, free = take(twos)

                def make(pe, b):
                    for f in range(FB):
                        cols = slice(f * P, (f + 1) * P)
                        last = three_passes(pe, ps[:, f * S:(f + 1) * S], g["w1_hi"][:, e0, cols],
                                            g["w1_lo"][:, e0, cols], x3_hi[:, :], x3_lo[:, :])
                    return last
                t_up[e0] = C("tensor", make, [parts_3, free])
                if e0 == NE - 1:
                    last_of["up"] = t_up[e0]

                def gelu(a, b):
                    for f in range(FB):
                        last = a.activation(hidden[e0 % 2][:, f, :], ps[:, f * S:(f + 1) * S], ACT.Gelu,
                                            bias=g["b1_sb"][:, e0 * FB + f:e0 * FB + f + 1])
                    return last
                t_gelu[e0] = C("scalar", gelu, [t_up[e0], t_down.get(e0 - 2)])
                free_up(twos, n, t_gelu[e0])

            up(0)
            yield "up0"
            n, ps6, free = take_small()

            def route(pe, b):
                for m in range(ST):
                    last = pe.matmul(ps6[:, m * NE:(m + 1) * NE], x3t[:, m * P:(m + 1) * P], g["wr"][:, :],
                                     start=True, stop=True)
                return last
            t = last_of["routed"] = C("tensor", route, [got_x3t, free])
            t = C("vector", lambda v, b: v.tensor_copy(
                logits[:, :, :].rearrange("p m e -> p (m e)"), ps6[:, 0:ST * NE]), [t])
            free_small(n, t)

            def largest(v, b):
                for m in range(ST):
                    last = v.max(top_v[:, m, :], logits[:, m, :])
                return last

            def places(v, b):
                for m in range(ST):
                    last = v.max_index(top_i[:, m, :], top_v[:, m, :], logits[:, m, :])
                return last
            t = plan.step("vector", "C", largest, [t], apart=True)
            t_i = plan.step("vector", "C", places, [t], apart=True)
            t = C("vector", lambda v, b: v.tensor_tensor(
                gate[:, 0, :], top_v[:, :, 1], top_v[:, :, 0], ALU.subtract), [t])
            t_e = C("gpsimd", lambda e, b: e.tensor_tensor(
                gate[:, 1, :], g["euler"][:, :], gate[:, 0, :], ALU.pow), [t])
            t_if = C("vector", lambda v, b: v.tensor_copy(top_if[:, :, :], top_i[:, :, 0:2]), [t_i])
            t = C("vector", lambda v, b: v.tensor_scalar(gate[:, 2, :], gate[:, 1, :], 1.0, None, ALU.add), [t_e])
            t = C("vector", lambda v, b: v.reciprocal(gate[:, 2, :], gate[:, 2, :]), [t])
            t = C("vector", lambda v, b: v.tensor_tensor(
                gate[:, 3, :], gate[:, 1, :], gate[:, 2, :], ALU.mult), [t])

            def weigh(v, b):
                for k in range(2):
                    for m in range(ST):
                        last = v.tensor_scalar(cw2[:, k, m, :], g["iota8"][:, :], top_if[:, m, k:k + 1],
                                               gate[:, 2 + k, m:m + 1], ALU.is_equal, ALU.mult)
                return last
            t = C("vector", weigh, [t, t_if])
            t_cw = C("vector", lambda v, b: v.tensor_tensor(
                cw[:, :, :], cw2[:, 0, :, :], cw2[:, 1, :, :], ALU.add), [t])
            yield "route"

            t_mix = [t_cw] * ST

            def down(e0):
                n, ps, free = take_small()

                def make(pe, b):
                    for m in range(ST):
                        for f in range(FB):
                            last = pe.matmul(ps[:, m * P:(m + 1) * P], hidden[e0 % 2][:, f, m * P:(m + 1) * P],
                                             g["w2_sb"][:, e0, f, :], start=(f == 0), stop=(f == FB - 1))
                    return last
                t_down[e0] = C("tensor", make, [t_gelu[e0], free])
                so_far = x3 if e0 == 0 else acc
                for m in range(ST):
                    t_mix[m] = C("vector", lambda v, b, m=m: v.scalar_tensor_tensor(
                        acc[:, m, :], ps[:, m * P:(m + 1) * P], cw[:, m, e0:e0 + 1], so_far[:, m, :],
                        ALU.mult, ALU.add), [t_down[e0], t_mix[m], got_x3])
                if e0 == 0:
                    last_of["x3 read"] = t_mix[ST - 1]
                free_small(n, t_mix[ST - 1])

            for e0 in range(NE):
                if e0 + 1 < NE:
                    up(e0 + 1)
                    yield f"up{e0 + 1}"
                down(e0)
                yield f"down{e0}"
                if e0 == 3:
                    n, ps7, free = take_small()

                    def turn_cw(pe, b):
                        for m in range(ST):
                            last = pe.transpose(ps7[0:NE, m * P:(m + 1) * P], cw[:, m, :], ident[:, :])
                        return last
                    t = C("tensor", turn_cw, [t_cw, free])
                    t_cwt = C("vector", lambda v, b: v.tensor_copy(cw_t[:, :], ps7[0:NE, 0:S]), [t])
                    free_small(n, t_cwt)
                    yield "turn_cw"
                if e0 == 4:
                    n, ps8, free = take_small()

                    def bias2(pe, b):
                        for m in range(ST):
                            last = pe.matmul(ps8[:, m * P:(m + 1) * P], cw_t[:, m * P:(m + 1) * P],
                                             g["b2_sb"][:, :], start=True, stop=True)
                        return last
                    t = C("tensor", bias2, [t_cwt, free])
                    t_mix = [C("vector", lambda v, b: v.tensor_tensor(
                        acc[:, :, :], ps8[:, 0:S].rearrange("p (m d) -> p m d", m=ST), acc[:, :, :], ALU.add),
                        [t, *t_mix])] * ST
                    free_small(n, t_mix[0])
                    yield "bias2"
            last_of["stored"] = plan.dma("gpsimd", "C", "out", lambda e, b: e.dma_start(
                g["out"][b].rearrange("(n p) d -> p n d", p=P), acc[:, :, :]), t_mix)

        running = {"W": once, "L": stage_l(), "A": stage_a(), "M": stage_m(), "B": stage_b(), "C": stage_c()}
        for stage, until in order:
            if stage in has or (stage == "W" and once):
                for label in running[stage]:
                    if label == until:
                        break
        for stage in has:
            assert next(running[stage], None) is None, stage
        queues = plan.queues
        plan.finish()
        return queues

    def segments_of():
        once = made_once(plan, sb_once, take, free_up, ones, twos, buffers, g)
        first = [(n - 3, iteration(has, ORDER[n], once)) for n, has in enumerate(("L", "LA", "LAMB"))]
        assert next(once, None) is None
        before_loop = [regions.last for regions in (ones, twos)]
        iteration("LAMBC", ORDER[3])
        for regions, last in zip((ones, twos), before_loop):
            regions.last = [a + b for a, b in zip(regions.last, last)]
        return first + [("loop", iteration("LAMBC", ORDER[3]))] + [
            (NB - left, iteration(has, ORDER[n])) for left, has, n in ((3, "AMBC", 3), (2, "MBC", 4), (1, "C", 4))]

    segments = segments_of()
    plan.per_batch.update(plan.once_counts)

    sems = {n: nc.alloc_semaphore(n) for n in plan.per_batch}
    ready = nc.alloc_semaphore("constants")

    with nc.Block() as block:
        def run(name):
            def body(eng):
                if name == "vector":
                    eng.memset(k_stack[64:96, :, :], 1.0).then_inc(ready, 1)
                    eng.memset(v_cols[:, :, :, :], 0.0).then_inc(ready, 1)
                    eng.wait_ge(ready, 2)
                    eng.memset(v_cols[:, :, :, DK:DK + 1], 1.0).then_inc(ready, 1)
                eng.wait_ge(ready, 3)
                for j, queues in segments:
                    queue = queues.get(name, [])
                    if not queue:
                        continue
                    if j == "loop":
                        for sem, n in plan.once_counts.items():
                            eng.wait_ge(sems[sem], n)
                        with eng.Fori(0, NB - 3) as reg:
                            plan.emit(eng, queue, sems, reg, True, g["spare"][:, :])
                    else:
                        plan.emit(eng, queue, sems, j, False)
                if name == "gpsimd":
                    eng.wait_ge(sems["dma_out"], NB * plan.per_batch["dma_out"])
            return body
        block.sync(run("sync"))
        block.gpsimd(run("gpsimd"))
        block.vector(run("vector"))
        block.scalar(run("scalar"))
        block.tensor(run("tensor"))


def kernel(x, ctx_1024, mask_BxSxS2_ik1, L0_attn_W_q, L0_attn_W_k, L0_attn_W_v, L0_attn_W_out, L0_xattn_Wq,
           L0_xattn_bq, L0_xattn_Wk, L0_xattn_bk, L0_xattn_Wv, L0_xattn_bv, L0_xattn_Wo, L0_xattn_bo,
           L0_ffn_w_router, L0_ffn_w1, L0_ffn_b1, L0_ffn_w2, L0_ffn_b2):
    import concourse.bacc as bacc
    from concourse.bass_utils import run_bass_kernel_spmd

    A = np.asarray
    by_pair = lambda w: A(w).reshape(NPAIR, P, D).transpose(1, 0, 2)
    turned = lambda w: A(w).reshape(NH, DK, D).transpose(2, 1, 0).reshape(D, P)
    arrays = {
        "x": A(x),
        "ctx_t": A(ctx_1024).reshape(NB * T2, D).T,
        "mask": A(mask_BxSxS2_ik1),
        "attn_w": np.stack([turned(L0_attn_W_q), turned(L0_attn_W_k), A(L0_attn_W_v).T, A(L0_attn_W_out).T], 1),
        "xq": by_pair(L0_xattn_Wq),
        "xk": by_pair(L0_xattn_Wk),
        "xv": by_pair(L0_xattn_Wv),
        "xo": A(L0_xattn_Wo).reshape(D, NPAIR, P).transpose(2, 1, 0),
        "xbias": np.stack([A(v).reshape(NPAIR, P).T for v in (L0_xattn_bq, L0_xattn_bk, L0_xattn_bv)], 1),
        "bo": A(L0_xattn_bo),
        "w_router": A(L0_ffn_w_router).T,
        "w1": A(L0_ffn_w1).transpose(2, 0, 1),
        "b1": A(L0_ffn_b1).reshape(NE * FB, P).T,
        "w2": A(L0_ffn_w2).reshape(NE, D, FB, P).transpose(3, 0, 2, 1),
        "b2": A(L0_ffn_b2),
    }
    arrays = {n: np.ascontiguousarray(a) for n, a in arrays.items()}
    nc = bacc.Bacc("TRN2", target_bir_lowering=False, num_devices=1)
    aps = {n: nc.dram_tensor(n, a.shape, mybir.dt.from_np(a.dtype), kind="ExternalInput").ap()
           for n, a in arrays.items()}
    out = nc.dram_tensor("out", (NB, S, D), F32, kind="ExternalOutput").ap()
    build(nc, *aps.values(), out)
    r = run_bass_kernel_spmd(nc, [arrays], core_ids=[0])
    return r.results[0]["out"]
```
